# Optimizing a Trainium2 kernel written in Bass

```python
import numpy as np
import jax
import jax.numpy as jnp

def _softmax(x, axis=-1):
    return jax.nn.softmax(x, axis=axis)

def _gelu(x):
    return jax.nn.gelu(x, approximate=True)

def _silu(x):
    return jax.nn.silu(x)

def _sigmoid(x):
    return jax.nn.sigmoid(x)

def _layernorm(x, axis=-1, eps=1e-05):
    m = jnp.mean(x, axis=axis, keepdims=True)
    v = jnp.var(x, axis=axis, keepdims=True)
    return (x - m) / jnp.sqrt(v + eps)

def _scatter_add(tgt, idx, src, axis=0):
    return tgt.at[idx].add(src)

def _segment_sum(src, seg, n):
    return jax.ops.segment_sum(src, seg, n)
kernel_name = 'mk_seq_preln_d1_jaxref_r4_f6ece6'

def setup_inputs(seed: int=0):
    np.random.seed(seed)
    _w = jnp.asarray

    def _L0_attn_setup():
        import jax, jax.numpy as jnp
        import numpy as np
        N_EMBD = 256
        BLOCK_SIZE = 512
        B = 8
        LN_EPS = 1e-05

        def _mlp(x, W1, b1, W2, b2):
            h = jax.nn.gelu(x @ W1 + b1, approximate=False)
            return h @ W2 + b2
        key = jax.random.key(seed)
        ks = jax.random.split(key, 14)
        C = N_EMBD
        std = 0.02
        d = {'x': jax.random.normal(ks[0], (B, BLOCK_SIZE, C), dtype=jnp.float32)}
        names = ['q', 'k', 'v']
        i = 1
        for n in names:
            d[f'W1{n}'] = jax.random.normal(ks[i], (C, C), dtype=jnp.float32) * std
            i += 1
            d[f'b1{n}'] = jnp.zeros((C,), dtype=jnp.float32)
            d[f'W2{n}'] = jax.random.normal(ks[i], (C, C), dtype=jnp.float32) * std
            i += 1
            d[f'b2{n}'] = jnp.zeros((C,), dtype=jnp.float32)
        d['ln_w'] = jnp.ones((C,), dtype=jnp.float32)
        d['ln_b'] = jnp.zeros((C,), dtype=jnp.float32)
        return d
    _L0_attn_in = _L0_attn_setup()

    def _L0_ffn_setup():
        import math
        import jax, jax.numpy as jnp
        import numpy as np
        D_CONTENT = 256
        D_POSITION = 32
        NUM_TILES = 8
        BATCH = 8
        SEQ = 512

        def make_pe(seq_len, d_pos):
            pos = jnp.arange(seq_len, dtype=jnp.float32)[:, None]
            div = jnp.exp(jnp.arange(0, d_pos, 2, dtype=jnp.float32) * (-math.log(10000.0) / d_pos))
            ang = pos * div
            pe = jnp.zeros((seq_len, d_pos), dtype=jnp.float32)
            pe = pe.at[:, 0::2].set(jnp.sin(ang))
            pe = pe.at[:, 1::2].set(jnp.cos(ang))
            return pe
        key = jax.random.key(seed)
        k1, k2, k3, k4 = jax.random.split(key, 4)
        x = jax.random.normal(k1, (BATCH, SEQ, D_CONTENT), dtype=jnp.float32)
        tile_sigs = jax.random.normal(k2, (NUM_TILES, D_POSITION), dtype=jnp.float32)
        lim = 1.0 / math.sqrt(D_CONTENT)
        W = jax.random.uniform(k3, (NUM_TILES, D_CONTENT, D_CONTENT), minval=-lim, maxval=lim, dtype=jnp.float32)
        b = jax.random.uniform(k4, (NUM_TILES, D_CONTENT), minval=-lim, maxval=lim, dtype=jnp.float32)
        return {'x': x, 'tile_sigs': tile_sigs, 'W': W, 'b': b}
    _L0_ffn_in = _L0_ffn_setup()
    _d = {'L0_attn_x': _L0_attn_in['x'], 'L0_attn_W1q': _L0_attn_in['W1q'], 'L0_attn_b1q': _L0_attn_in['b1q'], 'L0_attn_W2q': _L0_attn_in['W2q'], 'L0_attn_b2q': _L0_attn_in['b2q'], 'L0_attn_W1k': _L0_attn_in['W1k'], 'L0_attn_b1k': _L0_attn_in['b1k'], 'L0_attn_W2k': _L0_attn_in['W2k'], 'L0_attn_b2k': _L0_attn_in['b2k'], 'L0_attn_W1v': _L0_attn_in['W1v'], 'L0_attn_b1v': _L0_attn_in['b1v'], 'L0_attn_W2v': _L0_attn_in['W2v'], 'L0_attn_b2v': _L0_attn_in['b2v'], 'L0_attn_ln_w': _L0_attn_in['ln_w'], 'L0_attn_ln_b': _L0_attn_in['ln_b'], 'L0_ffn_tile_sigs': _L0_ffn_in['tile_sigs'], 'L0_ffn_W': _L0_ffn_in['W'], 'L0_ffn_b': _L0_ffn_in['b']}
    _x0 = _d['L0_attn_x']
    _d['L0_attn_x'] = jax.random.normal(jax.random.fold_in(jax.random.key(seed), 1), (2, 2048, 256), dtype=_x0.dtype)
    del _x0
    return _d

def reference(L0_attn_x, L0_attn_W1q, L0_attn_b1q, L0_attn_W2q, L0_attn_b2q, L0_attn_W1k, L0_attn_b1k, L0_attn_W2k, L0_attn_b2k, L0_attn_W1v, L0_attn_b1v, L0_attn_W2v, L0_attn_b2v, L0_attn_ln_w, L0_attn_ln_b, L0_ffn_tile_sigs, L0_ffn_W, L0_ffn_b):

    def _L0_attn_ref(x, W1q, b1q, W2q, b2q, W1k, b1k, W2k, b2k, W1v, b1v, W2v, b2v, ln_w, ln_b):
        import jax, jax.numpy as jnp
        import numpy as np
        N_EMBD = 256
        BLOCK_SIZE = 512
        B = 8
        LN_EPS = 1e-05

        def _mlp(x, W1, b1, W2, b2):
            h = jax.nn.gelu(x @ W1 + b1, approximate=False)
            return h @ W2 + b2
        Bsz, T, C = x.shape
        q = _mlp(x, W1q, b1q, W2q, b2q)
        k = _mlp(x, W1k, b1k, W2k, b2k)
        v = _mlp(x, W1v, b1v, W2v, b2v)
        scale = np.sqrt(N_EMBD * BLOCK_SIZE).astype(np.float32)
        scores = jnp.einsum('bid,bjd->bij', q, k) / scale
        mask = jnp.tril(jnp.ones((T, T), dtype=scores.dtype))
        scores = scores * mask
        out = jnp.einsum('bij,bjd->bid', scores, v)
        mu = jnp.mean(out, axis=-1, keepdims=True)
        var = jnp.mean(jnp.square(out - mu), axis=-1, keepdims=True)
        out = (out - mu) * jax.lax.rsqrt(var + LN_EPS) * ln_w + ln_b
        return out

    def _L0_ffn_ref(x, tile_sigs, W, b):
        import math
        import jax, jax.numpy as jnp
        import numpy as np
        D_CONTENT = 256
        D_POSITION = 32
        NUM_TILES = 8
        BATCH = 8
        SEQ = 512

        def make_pe(seq_len, d_pos):
            pos = jnp.arange(seq_len, dtype=jnp.float32)[:, None]
            div = jnp.exp(jnp.arange(0, d_pos, 2, dtype=jnp.float32) * (-math.log(10000.0) / d_pos))
            ang = pos * div
            pe = jnp.zeros((seq_len, d_pos), dtype=jnp.float32)
            pe = pe.at[:, 0::2].set(jnp.sin(ang))
            pe = pe.at[:, 1::2].set(jnp.cos(ang))
            return pe
        B, S, D = x.shape
        P = tile_sigs.shape[1]
        pe = make_pe(S, P)
        scores = jnp.einsum('sp,tp->st', pe, jnp.sign(tile_sigs))
        idx = jnp.argmax(scores, axis=-1)
        y_all = jnp.einsum('bsd,tod->bsto', x, W) + b
        idx4 = jnp.broadcast_to(idx[None, :, None, None], (B, S, 1, D))
        out = jnp.take_along_axis(y_all, idx4, axis=2)[:, :, 0]
        return out
    x = L0_attn_x
    x = x + _L0_attn_ref(_layernorm(x, axis=-1), L0_attn_W1q, L0_attn_b1q, L0_attn_W2q, L0_attn_b2q, L0_attn_W1k, L0_attn_b1k, L0_attn_W2k, L0_attn_b2k, L0_attn_W1v, L0_attn_b1v, L0_attn_W2v, L0_attn_b2v, L0_attn_ln_w, L0_attn_ln_b)
    x = x + _L0_ffn_ref(_layernorm(x, axis=-1), L0_ffn_tile_sigs, L0_ffn_W, L0_ffn_b)
    return x

_drawn_inputs = setup_inputs


def setup_inputs(seed=0):
    import zlib

    import numpy as np

    out = dict(_drawn_inputs(seed))
    spreads = {'L0_attn_b1q': (0.0, 0.1),
     'L0_attn_b2q': (0.0, 0.1),
     'L0_attn_b1k': (0.0, 0.1),
     'L0_attn_b2k': (0.0, 0.1),
     'L0_attn_b1v': (0.0, 0.1),
     'L0_attn_b2v': (0.0, 0.1),
     'L0_attn_ln_w': (1.0, 0.2),
     'L0_attn_ln_b': (0.0, 0.1)}
    factors = {}
    for name, (base, spread) in spreads.items():
        noise = np.random.default_rng([zlib.crc32(name.encode()), seed]).standard_normal(out[name].shape)
        drawn = base * np.exp(spread * noise) if base else spread * noise
        out[name] = jnp.asarray(drawn.astype(out[name].dtype))
    for name, factor in factors.items():
        out[name] = (out[name] * factor).astype(out[name].dtype)
    return out
```

```python
from contextlib import ExitStack

import concourse.bass as bass
from concourse import mybir

F32 = mybir.dt.float32
F32R = mybir.dt.float32r
I32 = mybir.dt.int32
ALU = mybir.AluOpType
ACT = mybir.ActivationFunctionType
AX_X = mybir.AxisListType.X

P = 128
NB = 2
T = 2048
C = 256
KC = C // P
GT = 512
CH = GT // P
STEPS = NB * T // GT
NT = 8
DP = 32
EPS = 1e-5
INV_SCALE = float((C * 512) ** -0.5)
NJ = T // P
ROW = C + 2
NBLK = (T + NT * (P - 1)) // P
FAR = 8192
FILLS = 18
SPLIT = ((0, 0), (0, 1), (1, 0))
Q, K, V = range(3)


def mk_seq_kernel(nc, x, w1, b1, w2, b2, ln_w, ln_b, sigs, ffn_w, ffn_b, pe, out):
    scratch = nc.dram_tensor("x1_rows", [T, NB * ROW], F32, kind="Internal").ap()
    rows_sbp = scratch.rearrange("(g c p) (b d) -> g b p c d", p=P, c=CH, b=NB)
    x_gbp = x.rearrange("b (g c p) d -> g b p c d", p=P, c=CH)
    out_rows = out.rearrange("b s d -> (b s) d")

    with ExitStack() as ctx:
        def sb(name, shape, dt=F32):
            return ctx.enter_context(nc.sbuf_tensor(name, shape, dt))

        def sem(name):
            return ctx.enter_context(nc.semaphore(name))

        w_stage = sb("w_stage", [P, 6, KC, C])
        w_all = sb("w_all", [P, NT, 2, KC * C], F32R)
        w_sp = w_all[:, 0:6].rearrange("p m a (k c) -> p m a k c", k=KC)
        wf_sp = w_all
        b1c = sb("b1c", [P, 3, KC])
        b2c = sb("b2c", [P, 2, KC])
        b2v_row = sb("b2v_row", [P, C])
        lnw_row = sb("lnw_row", [P, C])
        lnb_row = sb("lnb_row", [P, C])
        ident = sb("ident", [P, P])
        tril = sb("tril", [P, P])
        half = sb("half", [P, CH])
        xt = [sb(f"xt{b}", [P, CH, C]) for b in range(NB)]
        xres = [sb(f"xres{b}", [P, CH, ROW]) for b in range(NB)]
        xn = sb("xn", [P, CH, C])
        st1 = sb("st1", [P, CH, 6])
        mv1 = sb("mv1", [P, CH, 2])
        ve1 = sb("ve1", [P, CH])
        rs1 = sb("rs1", [P, CH])
        xnT = sb("xnT", [P, 2, KC, GT], F32R)
        h32 = sb("h32", [P, 6, GT])
        hT = sb("hT", [P, 6, 2, GT], F32R)
        qT = [sb(f"qT{b}", [P, 2, KC, GT], F32R) for b in range(NB)]
        kT = sb("kT", [P, 2, KC, GT], F32R)
        ktok = [sb(f"ktok{b}", [P, 2, CH, C], F32R) for b in range(NB)]
        v32 = sb("v32", [P, CH, C])
        vtok = [sb(f"vtok{b}", [P, 2, CH, C], F32R) for b in range(NB)]
        sc32 = sb("sc32", [P, GT])
        scT = sb("scT", [P, 2, GT], F32R)
        state = [sb(f"state{b}", [P, 2, KC * C], F32R) for b in range(NB)]
        cen = sb("cen", [P, CH, C])
        st2 = sb("st2", [P, CH, 6])
        mv2 = sb("mv2", [P, CH, 2])
        ve2 = sb("ve2", [P, CH])
        rs2 = sb("rs2", [P, CH])
        st3 = sb("st3", [P, CH, 6])
        mv3 = sb("mv3", [P, CH, 2])
        ve3 = sb("ve3", [P, CH])

        ring = [ctx.enter_context(nc.psum_tensor(f"ring{i}", [P, 512], F32)) for i in range(3)]
        sc_ps = ctx.enter_context(nc.psum_tensor("sc_ps", [P, 512], F32))
        o_ps = [ctx.enter_context(nc.psum_tensor(f"o_ps{i}", [P, 512], F32)) for i in range(2)]
        s_ps = [ctx.enter_context(nc.psum_tensor(f"s_ps{b}", [P, 512], F32)) for b in range(NB)]

        x_in = [sem(f"x_in{b}") for b in range(NB)]
        w_in = [sem(f"w_in{i}") for i in range(6)]
        small_in = sem("small_in")
        ffn_in = sem("ffn_in")
        route_in = sem("route_in")
        consts = sem("consts")
        zeroed = sem("zeroed")
        w_scaled = sem("w_scaled")
        w_hi = sem("w_hi")
        w_lo = sem("w_lo")
        stat1 = sem("stat1")
        aggr1 = sem("aggr1")
        var1 = sem("var1")
        rstd1 = sem("rstd1")
        xn_done = sem("xn_done")
        res_done = sem("res_done")
        fill = sem("fill")
        xnT_hi = sem("xnT_hi")
        xnT_lo = sem("xnT_lo")
        gelu = sem("gelu")
        h_hi_dve = sem("h_hi_dve")
        h_lo_dve = sem("h_lo_dve")
        h_hi_act = sem("h_hi_act")
        h_lo_pool = sem("h_lo_pool")
        qk_hi = sem("qk_hi")
        qk_lo = sem("qk_lo")
        v_sum = sem("v_sum")
        v_hi = sem("v_hi")
        v_lo = sem("v_lo")
        ktok_out = sem("ktok_out")
        scores = sem("scores")
        sc_mask = sem("sc_mask")
        sc_hi = sem("sc_hi")
        sc_lo = sem("sc_lo")
        o_ready = sem("o_ready")
        s_ready = sem("s_ready")
        s_hi = sem("s_hi")
        s_lo = sem("s_lo")
        o_stat = sem("o_stat")
        o_aggr = sem("o_aggr")
        o_cen = sem("o_cen")
        var2 = sem("var2")
        rstd2 = sem("rstd2")
        x1_made = sem("x1_made")
        stat3 = sem("stat3")
        aggr3 = sem("aggr3")
        var3 = sem("var3")
        rstd3 = sem("rstd3")
        x1_out = [sem(f"x1_out{b}") for b in range(NB)]

        sgn = sb("sgn", [DP, 3, NT])
        sig_in = sb("sig_in", [DP, NT])
        peT = [xt[i][0:DP, :, :].rearrange("p c d -> p (c d)") for i in range(2)]
        h_flat = h32[:, :, :].rearrange("p m n -> p (m n)")
        carved = [0]

        def carve(*dims, parts=P):
            n, at = 1, carved[0]
            for d in dims:
                n *= d
            carved[0] += n
            names = "abc"[:len(dims)]
            return h_flat[0:parts, at:at + n].rearrange(f"p ({' '.join(names)}) -> p {' '.join(names)}",
                                                        **dict(zip(names, dims)))

        rsc = carve(NT, NJ)
        rmax = sb("rmax", [P, NJ])
        req = carve(NT, NJ)
        rcand = carve(NT, NJ)
        rbest = sb("rbest", [P, NJ])
        onehot = carve(NT, NJ)
        lower = sb("lower", [P, P])
        ones = sb("ones", [P, P])
        revt = sb("revt", [P, NT, NJ])
        keep = sb("keep", [P, NT, NJ])
        tot = carve(NT, NJ)
        incl = carve(NT, NJ)
        zed = carve(NT, NJ)
        slot_t = carve(NT, NJ)
        slot = sb("slot", [P, NJ])
        blk_edge = sb("blk_edge", [P, NT, NJ])
        blk_gt = carve(NT, NJ)
        blks = sb("blks", [P, NT])
        ends = sb("ends", [P, NT])
        keep8 = sb("keep8", [P, NT])
        starts = sb("starts", [P, NT])
        kcol = sb("kcol", [1, NBLK, NT])
        kge = carve(NBLK, NT, parts=1)
        tile_f = sb("tile_f", [1, 2, NBLK])
        tile_i = sb("tile_i", [1, NBLK], I32)
        edges = sb("edges", [P, NJ, NBLK + 1])
        above = carve(NJ, NBLK + 1)
        inblk = carve(NJ, NBLK)
        posn = sb("posn", [P, NJ])
        poscol = carve(NJ, NBLK)
        nblk = sb("nblk", [P, NJ])
        rest = sb("rest", [P, NJ])
        lane = sb("lane", [P, P])
        lane_oh = [(xn if j < CH * KC else v32)[:, j // KC % CH, j % KC * P:j % KC * P + P] for j in range(NJ)]
        idx_f = sb("idx_f", [P, 5, NBLK])
        idx_i = sb("idx_i", [P, 3 * NBLK], I32)
        gidx = [sb(f"gidx{i}", [P, 1], I32) for i in range(2)]
        sidx = [sb(f"sidx{i}", [P, NB], I32) for i in range(2)]
        ffn_stage = w_stage[:, :, :, :].rearrange("p a k c -> p (a k c)")[:, 0:4 * 512].rearrange(
            "p (t k c) -> p t k c", t=4, k=KC)
        bias_rows = sb("bias_rows", [P, NT, C])
        grow = [xt[i][:, :, :].rearrange("p c d -> p (c d)")[:, 0:NB * ROW] for i in range(2)]
        xnb, resb, yb = [[h32[:, 2 * n + i, :].rearrange("p (b d) -> p b d", b=NB) for i in range(2)]
                         for n in range(3)]
        xbT = [hT[:, i] for i in range(2)]

        rconst = sem("rconst")
        rv = sem("rv")
        rp = sem("rp")
        wf_t = sem("wf_t")
        wf_hi = sem("wf_hi")
        wf_lo = sem("wf_lo")
        got = [sem(f"got{i}") for i in range(2)]
        sent = [sem(f"sent{i}") for i in range(2)]
        xnb_done = sem("xnb_done")
        resb_done = sem("resb_done")
        gidx_done = sem("gidx_done")
        xb_t = sem("xb_t")
        xb_hi = sem("xb_hi")
        xb_lo = sem("xb_lo")
        y_ps = sem("y_ps")
        y_done = sem("y_done")

        gate_dve = sem("gate_dve")
        gate_pool = sem("gate_pool")

        block = ctx.enter_context(nc.Block())

        def alone(eng, gate):
            eng.sem_inc(gate, 1)

        def cols(c):
            return slice(c * P, (c + 1) * P)

        @block.sync
        def _(sp):
            def load_x(g, b):
                sp.dma_start(xt[b][:, :, :], x_gbp[bass.ds(g, 1), b].rearrange("g p c d -> p (g c) d")
                             ).then_inc(x_in[b], 16)

            def store(g, b):
                sp.wait_ge(rstd3, NB * g + b + 1)
                sp.dma_start(rows_sbp[bass.ds(g, 1), b].rearrange("g p c d -> p (g c) d"), xres[b][:, :, :]
                             ).then_inc(x1_out[b], 16)

            load_x(0, 0)
            for i, w in enumerate((w1[Q], w1[K], w1[V], w2[Q], w2[K], w2[V])):
                sp.dma_start(w_stage[:, i, :, :], w.rearrange("(k p) n -> p k n", p=P)).then_inc(w_in[i], 16)
                if i == 0:
                    load_x(0, 1)
            sp.wait_ge(xn_done, 1)
            sp.wait_ge(res_done, 1)
            load_x(1, 0)
            sp.dma_start(bias_rows[:, :, :], ffn_b.partition_broadcast(P)).then_inc(route_in, 16)
            sp.dma_start(sig_in[:, :], sigs.rearrange("t d -> d t"), allow_slow_non_contiguous=True).then_inc(route_in, 16)

            def body(g, b, front, lead):
                if lead:
                    sp.wait_ge(xn_done, NB * g + b + 2)
                    sp.wait_ge(res_done, NB * g + b + 2)
                    load_x(g + 1 + b, 1 - b)
                store(g, b)

            with sp.Fori(0, STEPS // NB - 2) as g:
                for b in range(NB):
                    body(g, b, True, True)
            body(STEPS // NB - 2, 0, True, True)
            body(STEPS // NB - 2, 1, True, False)
            ffn_v = ffn_w.rearrange("t (k p) d -> p t k d", p=P)
            sp.wait_ge(w_lo, 6)
            sp.wait_ge(xn_done, STEPS)
            sp.wait_ge(res_done, STEPS)
            for i in range(2):
                sp.dma_start(peT[i], pe[:, i * T // 2:(i + 1) * T // 2]).then_inc(route_in, 16)
            sp.dma_start(ffn_stage, ffn_v[:, 0:4]).then_inc(ffn_in, 16)
            body(STEPS // NB - 1, 0, True, False)
            sp.wait_ge(wf_t, 4)
            sp.dma_start(ffn_stage, ffn_v[:, 4:8]).then_inc(ffn_in, 16)
            body(STEPS // NB - 1, 1, False, False)

        @block.tensor
        def _(te):
            def mm3(o, lhs, rhs, start=True, stop=True, check=False):
                n = len(lhs)
                for k in range(n):
                    for i, (a, c) in enumerate(SPLIT):
                        last = te.matmul(o, lhs[k][a], rhs[k][c], start=start and k == 0 and i == 0,
                                         stop=stop and k == n - 1 and i == 2, skip_group_check=check)
                return last

            def wpair(m, k, n0, n1):
                return [w_sp[:, m, a, k, n0:n1] for a in range(2)]

            def front_transposes(s, first):
                te.wait_ge(xn_done, s + 1)
                for k in range(KC):
                    if not first:
                        te.wait_ge(ktok_out, 4 * (s - 1) + 2 + k)
                    for c in range(CH):
                        last = te.transpose(ring[k][:, cols(c)], xn[:, c, cols(k)], ident[:, :])
                    last.then_inc(fill, 1)

            def front_h(s, ms, first):
                for m in ms:
                    if m == 0:
                        te.wait_ge(xnT_lo, 2 * s + 2)
                        if not first:
                            te.wait_ge(ktok_out, 4 * s)
                    if m >= 3:
                        te.wait_ge(gelu, 6 * s + m - 2)
                    if first and m % 2 == 0:
                        te.wait_ge(w_lo, m // 2 + 1)
                    mm3(ring[(2 + m) % 3][:, :], [wpair(m // 2, k, m % 2 * P, m % 2 * P + P) for k in range(KC)],
                        [[xnT[:, a, k, :] for a in range(2)] for k in range(KC)]).then_inc(fill, 1)

            def front_qk(s, which, first):
                for j in (2 * which, 2 * which + 1):
                    if j < 3:
                        te.wait_ge(gelu, 6 * s + 4 + j)
                    else:
                        te.wait_ge(qk_lo, 4 * s + 1)
                    if j % 2 == 0:
                        te.wait_ge(h_lo_dve, 3 * s + which + 1)
                        te.wait_ge(h_lo_pool, 3 * s + which + 1)
                        if first:
                            te.wait_ge(w_lo, 4 + which)
                    mm3(ring[(8 + j) % 3][:, :], [wpair(3 + which, k, j % 2 * P, j % 2 * P + P) for k in range(KC)],
                        [[hT[:, 2 * which + k, a, :] for a in range(2)] for k in range(KC)]).then_inc(fill, 1)

            def front_v(s, first):
                te.wait_ge(h_lo_dve, 3 * s + 3)
                te.wait_ge(h_lo_pool, 3 * s + 3)
                if first:
                    te.wait_ge(w_lo, 6)
                for j in range(2):
                    te.wait_ge(qk_lo, 4 * s + 2 + j)
                    for c in (2 * j, 2 * j + 1):
                        last = mm3(ring[j][:, c % 2 * C:c % 2 * C + C],
                                   [[hT[:, 4 + k, a, cols(c)] for a in range(2)] for k in range(KC)],
                                   [wpair(5, k, 0, C) for k in range(KC)])
                    last.then_inc(fill, 1)

            def front_scores(b, s):
                te.wait_ge(qk_lo, 4 * s + 4)
                te.wait_ge(sc_mask, s)
                for c in range(CH):
                    last = mm3(sc_ps[:, cols(c)], [[kT[:, a, k, cols(c)] for a in range(2)] for k in range(KC)],
                               [[qT[b][:, a, k, cols(c)] for a in range(2)] for k in range(KC)])
                last.then_inc(scores, 1)

            def front_ktok(s):
                for n in range(4):
                    if n == 0:
                        te.wait_ge(qk_lo, 4 * s + 4)
                    elif n < 3:
                        te.wait_ge(v_sum, 2 * s + n)
                    else:
                        te.wait_ge(ktok_out, 4 * s + 1)
                    for i in range(4):
                        c, k = 2 * (n // 2) + i // 2, i % 2
                        last = te.transpose(ring[(14 + n) % 3][:, cols(i)],
                                            kT[:, n % 2, k, cols(c)].bitcast(F32), ident[:, :])
                    last.then_inc(fill, 1)

            def back_chunk(b, s, c):
                te.wait_ge(s_lo, 4 * s + c + 1)
                te.wait_ge(o_cen, 4 * s + c + 1)
                if c == 0:
                    te.wait_ge(v_lo, 2 * s + 2)
                    te.wait_ge(sc_lo, s + 1)
                    te.wait_ge(ktok_out, 4 * s + 4)
                o = o_ps[c % 2][:, 0:C]
                mm3(o, [[qT[b][:, a, k, cols(c)] for a in range(2)] for k in range(KC)],
                    [[state[b][:, a, k * C:k * C + C] for a in range(2)] for k in range(KC)], stop=False)
                vs = [vtok[b][:, a, c, :] for a in range(2)]
                mm3(o, [[scT[:, a, cols(c)] for a in range(2)]], [vs], start=False).then_inc(o_ready, 1)
                for k in range(KC):
                    last = mm3(s_ps[b][:, k * C:k * C + C], [[ktok[b][:, a, c, cols(k)] for a in range(2)]], [vs],
                               start=False, check=True)
                last.then_inc(s_ready, 1)

            def body(g, b, front, lead, fillers=None):
                s = NB * g + b
                if front:
                    front_transposes(s + 1, False)
                back_chunk(b, s, 0)
                for c in range(1, CH):
                    if front:
                        front_h(s + 1, (2 * c - 2, 2 * c - 1), False)
                    elif fillers:
                        fillers(c - 1)
                    back_chunk(b, s, c)
                if front:
                    front_qk(s + 1, 0, False)
                    front_qk(s + 1, 1, False)
                    front_v(s + 1, False)
                    front_scores(1 - b, s + 1)
                    front_ktok(s + 1)

            te.wait_ge(consts, 2)
            front_transposes(0, True)
            te.wait_ge(zeroed, 2)
            front_h(0, range(6), True)
            front_qk(0, 0, True)
            front_qk(0, 1, True)
            front_v(0, True)
            front_scores(0, 0)
            front_ktok(0)
            with te.Fori(0, STEPS // NB - 1) as g:
                for b in range(NB):
                    body(g, b, True, True)
            body(STEPS // NB - 1, 0, True, False)

            def tile_weights(t):
                te.wait_ge(ffn_in, 16 * (t // 4 + 1))
                if t < 3:
                    te.wait_ge(ktok_out, 4 * STEPS)
                else:
                    te.wait_ge(wf_lo, t - 2)
                for k in range(KC):
                    for o in range(KC):
                        last = te.transpose(ring[t % 3][:, k * C + o * P:k * C + o * P + P],
                                            ffn_stage[:, t % 4, o, cols(k)], ident[:, :])
                last.then_inc(wf_t, 1)

            def route_scores():
                te.wait_ge(rv, 3)
                te.wait_ge(route_in, 64)
                te.wait_ge(sc_mask, STEPS)
                for j in range(NJ):
                    last = te.matmul(sc_ps[:, j * NT:j * NT + NT], peT[j // 8][:, cols(j % 8)], sgn[:, 2, :],
                                     start=True, stop=True)
                last.then_inc(rp, 1)

            def route_counts():
                te.wait_ge(rv, 9)
                te.wait_ge(rconst, 8)
                oh = onehot[:, :, :].rearrange("p t j -> p (t j)")
                te.matmul(sc_ps[:, 128:256], lower[:, :], oh, start=True, stop=True)
                te.matmul(sc_ps[:, 256:384], ones[:, :], oh, start=True, stop=True).then_inc(rp, 1)

            def route_invert():
                te.wait_ge(rv, 26)
                for j in range(NJ):
                    te.wait_ge(rv, 27 + j)
                    last = te.matmul(sc_ps[:, 0:NBLK], lane_oh[j], poscol[:, j, :], start=(j == 0),
                                     stop=(j == NJ - 1))
                last.then_inc(rp, 1)

            def fillers(n):
                if n == 0:
                    route_scores()
                    for t in range(0, 2):
                        tile_weights(t)
                if n == 1:
                    route_counts()
                    for t in range(2, 4):
                        tile_weights(t)
                if n == 2:
                    route_invert()

            body(STEPS // NB - 1, 1, False, False, fillers)
            for t in range(4, NT):
                tile_weights(t)

            def blk(n, p, first):
                te.wait_ge(xnb_done, n + 1)
                if not first:
                    te.wait_ge(xb_lo, n - 1)
                for b in range(NB):
                    for k in range(KC):
                        last = te.transpose(ring[p][:, b * C + k * P:b * C + k * P + P], xnb[p][:, b, cols(k)],
                                            ident[:, :])
                last.then_inc(xb_t, 1)
                t = te.value_load(tile_i[0:1, bass.ds(n, 1)], min_val=0, max_val=NT - 1)
                te.wait_ge(xb_lo, n + 1)
                if not first:
                    te.wait_ge(y_done, n - 1)
                for b in range(NB):
                    last = mm3(o_ps[p][:, b * C:b * C + C],
                               [[xbT[p][:, a, b * C + k * P:b * C + k * P + P] for a in range(2)] for k in range(KC)],
                               [[wf_sp[:, bass.ds(t, 1), a, k * C:k * C + C].rearrange("p t c -> p (t c)")
                                 for a in range(2)] for k in range(KC)])
                last.then_inc(y_ps, 1)

            te.wait_ge(wf_lo, NT)
            te.wait_ge(rv, 49)
            te.wait_ge(o_cen, 4 * STEPS + 2)
            blk(0, 0, True)
            blk(1, 1, True)
            blk(2, 0, False)
            with te.Fori(0, (NBLK - 3) // 2) as i:
                blk(2 * i + 3, 1, False)
                blk(2 * i + 4, 0, False)

        @block.scalar
        def _(act):
            for i in range(3):
                act.dma_start(b1c[:, i, :], b1[i].rearrange("(k p) -> p k", p=P),
                              allow_slow_non_contiguous=True).then_inc(small_in, 16)
            for i in range(2):
                act.dma_start(b2c[:, i, :], b2[i].rearrange("(k p) -> p k", p=P),
                              allow_slow_non_contiguous=True).then_inc(small_in, 16)
            act.dma_start(lnb_row[:, :], ln_b.partition_broadcast(P)).then_inc(small_in, 16)
            act.dma_start(lnw_row[:, :], ln_w.partition_broadcast(P)).then_inc(small_in, 16)
            act.dma_start(b2v_row[:, :], b2[V].partition_broadcast(P)).then_inc(small_in, 16)

            def xnT_rounded(s):
                for k in range(KC):
                    act.wait_ge(fill, FILLS * s + 1 + k)
                    nc.scalar.copy(xnT[:, 0, k, :], ring[k][:, :]).then_inc(xnT_hi, 1)

            def gelus(s, ms):
                for m in ms:
                    act.wait_ge(fill, FILLS * s + 3 + m)
                    nc.scalar.activation(h32[:, m, :], ring[(2 + m) % 3][:, :], ACT.Gelu,
                                         bias=b1c[:, m // 2, m % 2:m % 2 + 1]).then_inc(gelu, 1)

            def h_rounded(s, m):
                act.wait_ge(gelu, 6 * s + m + 1)
                nc.scalar.copy(hT[:, m, 0, :], h32[:, m, :]).then_inc(h_hi_act, 1)

            def qk_rounded(b, s):
                for j in range(4):
                    act.wait_ge(fill, FILLS * s + 9 + j)
                    nc.scalar.activation((qT[b] if j < 2 else kT)[:, 0, j % 2, :], ring[(8 + j) % 3][:, :],
                                         ACT.Identity, bias=b2c[:, j // 2, j % 2:j % 2 + 1]).then_inc(qk_hi, 1)

            def v_rounded(b, s):
                for j in range(2):
                    act.wait_ge(v_sum, 2 * s + 1 + j)
                    nc.scalar.copy(vtok[b][:, 0, 2 * j:2 * j + 2, :], v32[:, 2 * j:2 * j + 2, :]).then_inc(v_hi, 1)

            def scores_rounded(s):
                act.wait_ge(sc_mask, s + 1)
                nc.scalar.copy(scT[:, 0, :], sc32[:, :]).then_inc(sc_hi, 1)

            def ktok_copied(b, s):
                for n in range(4):
                    act.wait_ge(fill, FILLS * s + 15 + n)
                    nc.scalar.copy(ktok[b][:, n % 2, 2 * (n // 2):2 * (n // 2) + 2, :],
                                   ring[(14 + n) % 3][:, :].rearrange("p (c d) -> p c d", c=2)
                                   ).then_inc(ktok_out, 1)

            def state_rounded(b, s, c):
                act.wait_ge(s_ready, 4 * s + c + 1)
                nc.scalar.copy(state[b][:, 0, :], s_ps[b][:, :]).then_inc(s_hi, 1)

            def tile_rounded(ts):
                for t in ts:
                    act.wait_ge(wf_t, t + 1)
                    nc.scalar.copy(wf_sp[:, t, 0, :], ring[t % 3][:, :]).then_inc(wf_hi, 1)

            def body(g, b, front, lead, fillers=None):
                s = NB * g + b
                if front:
                    xnT_rounded(s + 1)
                state_rounded(b, s, 0)
                for c in range(1, CH):
                    if front:
                        gelus(s + 1, (2 * c - 2, 2 * c - 1))
                        if c > 1:
                            h_rounded(s + 1, 2 * c - 3)
                    elif fillers:
                        fillers(c - 1)
                    state_rounded(b, s, c)
                if front:
                    h_rounded(s + 1, 5)
                    qk_rounded(1 - b, s + 1)
                    v_rounded(1 - b, s + 1)
                    scores_rounded(s + 1)
                    ktok_copied(1 - b, s + 1)

            for i in range(6):
                if i < 3:
                    act.wait_ge(w_in[i], 16)
                else:
                    act.wait_ge(w_scaled, 1)
                    act.wait_ge(w_in[i], 16)
                nc.scalar.copy(w_sp[:, i, 0, :, :], w_stage[:, i, :, :]).then_inc(w_hi, 1)
                if i == 1:
                    xnT_rounded(0)
            act.wait_ge(small_in, 16 * 8)
            gelus(0, range(6))
            for m in (1, 3, 5):
                h_rounded(0, m)
            qk_rounded(0, 0)
            v_rounded(0, 0)
            scores_rounded(0)
            ktok_copied(0, 0)
            with act.Fori(0, STEPS // NB - 1) as g:
                for b in range(NB):
                    body(g, b, True, True)
            body(STEPS // NB - 1, 0, True, False)

            def fillers(n):
                if n < 2:
                    tile_rounded((2 * n, 2 * n + 1))

            body(STEPS // NB - 1, 1, False, False, fillers)
            tile_rounded(range(4, NT))

            def blk(n, p):
                act.wait_ge(xb_t, n + 1)
                nc.scalar.copy(xbT[p][:, 0, :], ring[p][:, :]).then_inc(xb_hi, 1)

            blk(0, 0)
            with act.Fori(0, (NBLK - 1) // 2) as i:
                blk(2 * i + 1, 1)
                blk(2 * i + 2, 0)

        @block.vector
        def _(dve):
            def lead_stats(g, b):
                s = NB * g + b
                dve.wait_ge(x_in[b], 16 * (g + 1))
                for c in range(CH):
                    last = nc.vector.bn_stats(st1[:, c, :], xt[b][:, c, :])
                last.then_inc(stat1, 1)
                dve.wait_ge(stat1, s + 1)
                alone(dve, gate_dve)
                for c in range(CH):
                    last = nc.vector.bn_aggr(mv1[:, c, :], st1[:, c, :])
                last.then_inc(aggr1, 1)
                dve.wait_ge(aggr1, s + 1)
                nc.vector.tensor_scalar(ve1[:, :], mv1[:, :, 1], EPS, None, ALU.add).then_inc(var1, 1)

            def lead_norm(g, b, first):
                s = NB * g + b
                dve.wait_ge(rstd1, s + 1)
                if not first:
                    dve.wait_ge(fill, FILLS * (s - 1) + 2)
                for c in range(CH):
                    last = nc.vector.tensor_scalar(xn[:, c, :], xt[b][:, c, :], mv1[:, c, 0:1], rs1[:, c:c + 1],
                                                   ALU.subtract, ALU.mult)
                last.then_inc(xn_done, 1)

            def xnT_rest(s):
                for k in range(KC):
                    dve.wait_ge(xnT_hi, 2 * s + 1 + k)
                    nc.vector.tensor_tensor(xnT[:, 1, k, :], ring[k][:, :], xnT[:, 0, k, :].bitcast(F32),
                                            ALU.subtract).then_inc(xnT_lo, 1)

            def h_split(s, m):
                dve.wait_ge(gelu, 6 * s + m + 1)
                nc.vector.tensor_copy(hT[:, m, 0, :], h32[:, m, :]).then_inc(h_hi_dve, 1)
                dve.wait_ge(h_hi_dve, 3 * s + m // 2 + 1)
                nc.vector.tensor_tensor(hT[:, m, 1, :], h32[:, m, :], hT[:, m, 0, :].bitcast(F32),
                                        ALU.subtract).then_inc(h_lo_dve, 1)

            def qk_rest(b, s):
                for j in range(4):
                    d = qT[b] if j < 2 else kT
                    dve.wait_ge(qk_hi, 4 * s + 1 + j)
                    nc.vector.scalar_tensor_tensor(out=d[:, 1, j % 2, :], in0=ring[(8 + j) % 3][:, :],
                                                   scalar=b2c[:, j // 2, j % 2:j % 2 + 1],
                                                   in1=d[:, 0, j % 2, :].bitcast(F32),
                                                   op0=ALU.add, op1=ALU.subtract).then_inc(qk_lo, 1)

            def v_biased(s):
                for j in range(2):
                    dve.wait_ge(fill, FILLS * s + 13 + j)
                    nc.vector.tensor_tensor(v32[:, 2 * j:2 * j + 2, :], ring[j][:, :].rearrange("p (c d) -> p c d", c=2),
                                            b2v_row[:, :].unsqueeze(1).broadcast_to([P, 2, C]),
                                            ALU.add).then_inc(v_sum, 1)

            def scores_masked(s):
                dve.wait_ge(scores, s + 1)
                nc.vector.tensor_tensor(sc32[:, :].rearrange("p (c i) -> p c i", c=CH),
                                        sc_ps[:, :].rearrange("p (c i) -> p c i", c=CH),
                                        tril[:, :].unsqueeze(1).broadcast_to([P, CH, P]), ALU.mult).then_inc(sc_mask, 1)
                dve.wait_ge(sc_hi, s + 1)
                nc.vector.tensor_tensor(scT[:, 1, :], sc32[:, :], scT[:, 0, :].bitcast(F32),
                                        ALU.subtract).then_inc(sc_lo, 1)

            def state_rest(b, s, c):
                dve.wait_ge(s_hi, 4 * s + c + 1)
                nc.vector.tensor_tensor(state[b][:, 1, :], s_ps[b][:, :], state[b][:, 0, :].bitcast(F32),
                                        ALU.subtract).then_inc(s_lo, 1)

            def out_centred(s, c):
                o = o_ps[c % 2][:, 0:C]
                dve.wait_ge(o_ready, 4 * s + c + 1)
                nc.vector.bn_stats(st2[:, c, :], o).then_inc(o_stat, 1)
                dve.wait_ge(o_stat, 4 * s + c + 1)
                alone(dve, gate_dve)
                nc.vector.bn_aggr(mv2[:, c, :], st2[:, c, :]).then_inc(o_aggr, 1)
                dve.wait_ge(o_aggr, 4 * s + c + 1)
                nc.vector.scalar_tensor_tensor(out=cen[:, c, :], in0=o, scalar=mv2[:, c, 0:1], in1=lnw_row[:, :],
                                               op0=ALU.subtract, op1=ALU.mult).then_inc(o_cen, 1)

            def out_var(s):
                nc.vector.tensor_scalar(ve2[:, :], mv2[:, :, 1], EPS, None, ALU.add).then_inc(var2, 1)

            def x1_final(g, b):
                s = NB * g + b
                dve.wait_ge(rstd2, s + 1)
                dve.wait_ge(res_done, s + 1)
                for c in range(CH):
                    last = nc.vector.scalar_tensor_tensor(out=xres[b][:, c, 0:C], in0=cen[:, c, :],
                                                          scalar=rs2[:, c:c + 1], in1=xres[b][:, c, 0:C],
                                                          op0=ALU.mult, op1=ALU.add)
                last.then_inc(x1_made, 1)
                dve.wait_ge(x1_made, s + 1)
                for c in range(CH):
                    last = nc.vector.bn_stats(st3[:, c, :], xres[b][:, c, 0:C])
                last.then_inc(stat3, 1)
                dve.wait_ge(stat3, s + 1)
                alone(dve, gate_dve)
                for c in range(CH):
                    last = nc.vector.bn_aggr(mv3[:, c, :], st3[:, c, :])
                last.then_inc(aggr3, 1)
                dve.wait_ge(aggr3, s + 1)
                nc.vector.tensor_copy(xres[b][:, :, C], mv3[:, :, 0])
                nc.vector.tensor_scalar(ve3[:, :], mv3[:, :, 1], EPS, None, ALU.add).then_inc(var3, 1)

            def body(g, b, front, lead, fillers=None):
                s = NB * g + b
                if front:
                    xnT_rest(s + 1)
                state_rest(b, s, 0)
                out_centred(s, 0)
                for c in range(1, CH):
                    if front:
                        h_split(s + 1, 2 * c - 2)
                    elif fillers:
                        fillers(c - 1)
                    state_rest(b, s, c)
                    out_centred(s, c)
                out_var(s)
                if lead:
                    lead_stats(g + 1, b)
                if front:
                    qk_rest(1 - b, s + 1)
                x1_final(g, b)
                if front:
                    v_biased(s + 1)
                    scores_masked(s + 1)
                if lead:
                    lead_norm(g + 1, b, False)

            for b in range(NB):
                nc.vector.memset(s_ps[b][:, :], 0.0).then_inc(zeroed, 1)
            for b in range(NB):
                last = nc.vector.memset(state[b][:, :, :].bitcast(F32), 0.0)
            last.then_inc(s_lo, 1)
            dve.sem_inc(o_cen, 2)
            lead_stats(0, 0)
            lead_norm(0, 0, True)

            def weights_rest(ws):
                for i in ws:
                    dve.wait_ge(w_hi, i + 1)
                    nc.vector.tensor_tensor(w_sp[:, i, 1, :, :], w_stage[:, i, :, :],
                                            w_sp[:, i, 0, :, :].bitcast(F32), ALU.subtract).then_inc(w_lo, 1)

            dve.wait_ge(w_in[3], 16)
            nc.vector.tensor_scalar(w_stage[:, 3, :, :], w_stage[:, 3, :, :], INV_SCALE, None,
                                    ALU.mult).then_inc(w_scaled, 1)
            weights_rest((0, 1))
            xnT_rest(0)
            weights_rest((2, 3, 4, 5))
            dve.wait_ge(small_in, 16 * 8)
            nc.vector.tensor_scalar(b2c[:, Q, :], b2c[:, Q, :], INV_SCALE, None, ALU.mult).then_inc(w_scaled, 1)
            lead_stats(0, 1)
            for m in (0, 2, 4):
                h_split(0, m)
            dve.wait_ge(w_scaled, 2)
            qk_rest(0, 0)
            v_biased(0)
            dve.wait_ge(consts, 4)
            scores_masked(0)
            lead_norm(0, 1, False)
            with dve.Fori(0, STEPS // NB - 1) as g:
                for b in range(NB):
                    body(g, b, True, True)
            body(STEPS // NB - 1, 0, True, False)

            done = [0]

            def link(ins):
                done[0] += 1
                ins.then_inc(rv, 1)
                dve.wait_ge(rv, done[0])

            def tile_rest(ts):
                for t in ts:
                    dve.wait_ge(wf_hi, t + 1)
                    nc.vector.tensor_tensor(wf_sp[:, t, 1, :], ring[t % 3][:, :], wf_sp[:, t, 0, :].bitcast(F32),
                                            ALU.subtract).then_inc(wf_lo, 1)

            def over_t(a):
                return a.unsqueeze(1).broadcast_to([P, NT, NJ])

            def over_j(a):
                return a.unsqueeze(2).broadcast_to([P, NT, NJ])

            def by_j(a):
                return a.rearrange("p t j -> p j t")

            def route_signs():
                dve.wait_ge(route_in, 64)
                link(nc.vector.tensor_scalar(sgn[:, 0, :], sig_in[:, :], 0.0, None, ALU.is_gt))
                link(nc.vector.tensor_scalar(sgn[:, 1, :], sig_in[:, :], 0.0, None, ALU.is_lt))
                link(nc.vector.tensor_tensor(sgn[:, 2, :], sgn[:, 0, :], sgn[:, 1, :], ALU.subtract))

            def route_argmax():
                dve.wait_ge(rp, 1)
                dve.wait_ge(rconst, 8)
                link(nc.vector.tensor_copy(rsc[:, :, :], sc_ps[:, 0:NJ * NT].rearrange("p (j t) -> p t j", t=NT)))
                link(nc.vector.tensor_reduce(rmax[:, :], by_j(rsc[:, :, :]), AX_X, ALU.max))
                link(nc.vector.tensor_tensor(req[:, :, :], rsc[:, :, :], over_t(rmax[:, :]), ALU.is_ge))
                link(nc.vector.tensor_tensor(rcand[:, :, :], req[:, :, :], revt[:, :, :], ALU.mult))
                link(nc.vector.tensor_reduce(rbest[:, :], by_j(rcand[:, :, :]), AX_X, ALU.max))
                link(nc.vector.tensor_tensor(onehot[:, :, :], revt[:, :, :], over_t(rbest[:, :]), ALU.is_equal))

            def route_slots():
                dve.wait_ge(rp, 2)
                link(nc.vector.tensor_copy(tot[:, :, :], sc_ps[:, 256:384].rearrange("p (t j) -> p t j", t=NT)))
                link(nc.vector.tensor_tensor_scan(incl[:, :, :].rearrange("p t j -> p (t j)"),
                                                  keep[:, :, :].rearrange("p t j -> p (t j)"),
                                                  tot[:, :, :].rearrange("p t j -> p (t j)"), 0.0,
                                                  ALU.mult, ALU.add))
                link(nc.vector.tensor_tensor(blk_gt[:, :, :], over_j(incl[:, :, NJ - 1]), blk_edge[:, :, :],
                                             ALU.is_gt))
                link(nc.vector.tensor_reduce(blks[:, :], blk_gt[:, :, :], AX_X, ALU.add))
                link(nc.vector.tensor_tensor_scan(ends[:, :], keep8[:, :], blks[:, :], 0.0, ALU.mult, ALU.add))
                link(nc.vector.tensor_tensor(starts[:, :], ends[:, :], blks[:, :], ALU.subtract))
                link(nc.vector.tensor_scalar(starts[:, :], starts[:, :], float(P), None, ALU.mult))
                link(nc.vector.tensor_tensor(zed[:, :, :], incl[:, :, :], tot[:, :, :], ALU.subtract))
                link(nc.vector.tensor_tensor(zed[:, :, :], zed[:, :, :], over_j(starts[:, :]), ALU.add))
                link(nc.vector.tensor_tensor(zed[:, :, :], sc_ps[:, 128:256].rearrange("p (t j) -> p t j", t=NT),
                                             zed[:, :, :], ALU.add))
                link(nc.vector.tensor_tensor(slot_t[:, :, :], zed[:, :, :], onehot[:, :, :], ALU.mult))
                link(nc.vector.tensor_reduce(slot[:, :], by_j(slot_t[:, :, :]), AX_X, ALU.add))
                link(nc.vector.tensor_tensor(above[:, :, :], slot[:, :].unsqueeze(2).broadcast_to([P, NJ, NBLK + 1]),
                                             edges[:, :, :], ALU.is_ge))
                link(nc.vector.tensor_tensor(inblk[:, :, :], above[:, :, 0:NBLK], above[:, :, 1:NBLK + 1],
                                             ALU.subtract))
                link(nc.vector.tensor_tensor(poscol[:, :, :], inblk[:, :, :],
                                             posn[:, :].unsqueeze(2).broadcast_to([P, NJ, NBLK]), ALU.mult))
                link(nc.vector.tensor_reduce(nblk[:, :], above[:, :, 1:NBLK], AX_X, ALU.add))
                link(nc.vector.scalar_tensor_tensor(out=rest[:, :], in0=nblk[:, :], scalar=-float(P), in1=slot[:, :],
                                                    op0=ALU.mult, op1=ALU.add))
                for j in range(NJ):
                    done[0] += 1
                    nc.vector.tensor_scalar(lane_oh[j], lane[:, :], rest[:, j:j + 1], None,
                                            ALU.is_equal).then_inc(rv, 1)

            def route_tables():
                link(nc.vector.tensor_tensor(kge[:, :, :], kcol[:, :, :],
                                             ends[0:1, :].unsqueeze(1).broadcast_to([1, NBLK, NT]), ALU.is_ge))
                link(nc.vector.tensor_reduce(tile_f[:, 0, :], kge[:, :, :], AX_X, ALU.add))
                link(nc.vector.tensor_scalar(tile_f[:, 1, :], tile_f[:, 0, :], float(NT - 1), None, ALU.min))
                link(nc.vector.tensor_copy(tile_i[:, :], tile_f[:, 1, :]))
                dve.wait_ge(rp, 3)
                link(nc.vector.tensor_copy(idx_f[:, 0, :], sc_ps[:, 0:NBLK]))
                link(nc.vector.tensor_scalar(idx_f[:, 1, :], idx_f[:, 0, :], -1.0, 0.0, ALU.add, ALU.max))
                link(nc.vector.tensor_scalar(idx_f[:, 2, :], idx_f[:, 0, :], 0.0, float(FAR), ALU.is_equal, ALU.mult))
                link(nc.vector.scalar_tensor_tensor(out=idx_f[:, 3, :], in0=idx_f[:, 0, :], scalar=-1.0,
                                                    in1=idx_f[:, 2, :], op0=ALU.add, op1=ALU.add))
                link(nc.vector.tensor_scalar(idx_f[:, 4, :], idx_f[:, 3, :], float(T), None, ALU.add))
                link(nc.vector.tensor_copy(idx_i[:, 0:NBLK], idx_f[:, 1, :]))
                link(nc.vector.tensor_copy(idx_i[:, NBLK:3 * NBLK].rearrange("p (b k) -> p b k", b=NB), idx_f[:, 3:5, :]))

            def fillers(n):
                if n == 0:
                    route_argmax()
                    tile_rest((0, 1))
                if n == 1:
                    route_slots()
                    tile_rest((2, 3))
                if n == 2:
                    route_tables()

            route_signs()
            body(STEPS // NB - 1, 1, False, False, fillers)
            tile_rest(range(4, NT))

            def blk(n, half_n, p, first):
                t = dve.value_load(tile_i[0:1, bass.ds(n, 1)], min_val=0, max_val=NT - 1)
                dve.wait_ge(got[p], 16 * half_n + 16)
                if not first:
                    dve.wait_ge(xb_t, n - 1)
                for b in range(NB):
                    r = grow[p][:, b * ROW:(b + 1) * ROW]
                    last = nc.vector.tensor_scalar(xnb[p][:, b, :], r[:, 0:C], r[:, C:C + 1], r[:, C + 1:C + 2],
                                                   ALU.subtract, ALU.mult)
                last.then_inc(xnb_done, 1)
                if not first:
                    dve.wait_ge(y_done, n - 1)
                nc.vector.tensor_tensor(resb[p],
                                        grow[p].rearrange("p (b d) -> p b d", b=NB)[:, :, 0:C],
                                        bias_rows[:, bass.ds(t, 1), :].broadcast_to([P, NB, C]),
                                        ALU.add).then_inc(resb_done, 1)
                nc.vector.tensor_copy(gidx[p][:, :], idx_i[:, bass.ds(n + 2, 1)]).then_inc(gidx_done, 1)

            def blk_end(n, half_n, p, first):
                dve.wait_ge(xb_hi, n + 1)
                nc.vector.tensor_tensor(xbT[p][:, 1, :], ring[p][:, :], xbT[p][:, 0, :].bitcast(F32),
                                        ALU.subtract).then_inc(xb_lo, 1)

            def blk_out(n, half_n, p, first):
                dve.wait_ge(y_ps, n + 1)
                dve.wait_ge(resb_done, n + 1)
                if not first:
                    dve.wait_ge(sent[p], 32 * half_n)
                nc.vector.tensor_copy(sidx[p][:, :], idx_i[:, NBLK:3 * NBLK].rearrange("p (b k) -> p b k", b=NB)
                                      [:, :, bass.ds(n, 1)].rearrange("p b k -> p (b k)"))
                nc.vector.tensor_tensor(yb[p].rearrange("p b d -> p (b d)"), o_ps[p][:, :],
                                        resb[p].rearrange("p b d -> p (b d)"),
                                        ALU.add).then_inc(y_done, 1)

            blk(0, 0, 0, True)
            blk_end(0, 0, 0, True)
            blk(1, 0, 1, True)
            blk_out(0, 0, 0, True)
            blk_end(1, 0, 1, True)
            blk(2, 1, 0, False)
            blk_out(1, 0, 1, True)
            with dve.Fori(0, (NBLK - 3) // 2) as i:
                blk_end(2 * i + 2, i + 1, 0, False)
                blk(2 * i + 3, i + 1, 1, False)
                blk_out(2 * i + 2, i + 1, 0, False)
                blk_end(2 * i + 3, i + 1, 1, False)
                blk(2 * i + 4, i + 2, 0, False)
                blk_out(2 * i + 3, i + 1, 1, False)
            blk_end(NBLK - 1, NBLK // 2, 0, False)
            blk_out(NBLK - 1, NBLK // 2, 0, False)

        @block.gpsimd
        def _(pool):
            nc.gpsimd.memset(ident[:, :], 0.0).then_inc(consts, 1)
            pool.wait_ge(consts, 1)
            nc.gpsimd.affine_select(out=ident[:, :], in_=ident[:, :], compare_op=ALU.not_equal, fill=1.0, base=0,
                                    pattern=[[-1, P]], channel_multiplier=1).then_inc(consts, 1)
            nc.gpsimd.memset(half[:, :], -0.5).then_inc(consts, 1)
            nc.gpsimd.memset(tril[:, :], 1.0).then_inc(rconst, 1)
            pool.wait_ge(rconst, 1)

            def rstd_lead(s):
                pool.wait_ge(var1, s + 1)
                nc.gpsimd.tensor_tensor(rs1[:, :], ve1[:, :], half[:, :], ALU.pow).then_inc(rstd1, 1)

            def residual(g, b, first):
                pool.wait_ge(x_in[b], 16 * (g + 1))
                if not first:
                    pool.wait_ge(x1_out[b], 16 * g)
                nc.gpsimd.tensor_tensor(xres[b][:, :, 0:C], xt[b][:, :, :],
                                        lnb_row[:, :].unsqueeze(1).broadcast_to([P, CH, C]),
                                        ALU.add).then_inc(res_done, 1)

            def h_rest(s, m):
                pool.wait_ge(h_hi_act, 3 * s + m // 2 + 1)
                nc.gpsimd.tensor_tensor(hT[:, m, 1, :], h32[:, m, :], hT[:, m, 0, :].bitcast(F32),
                                        ALU.subtract).then_inc(h_lo_pool, 1)

            def v_rest(b, s):
                for j in range(2):
                    pool.wait_ge(v_hi, 2 * s + 1 + j)
                    nc.gpsimd.tensor_tensor(vtok[b][:, 1, 2 * j:2 * j + 2, :], v32[:, 2 * j:2 * j + 2, :],
                                            vtok[b][:, 0, 2 * j:2 * j + 2, :].bitcast(F32),
                                            ALU.subtract).then_inc(v_lo, 1)

            def rstd_out(s):
                pool.wait_ge(var2, s + 1)
                nc.gpsimd.tensor_tensor(rs2[:, :], ve2[:, :], half[:, :], ALU.pow).then_inc(rstd2, 1)

            def rstd_x1(b, s):
                pool.wait_ge(var3, s + 1)
                nc.gpsimd.tensor_tensor(xres[b][:, :, C + 1], ve3[:, :], half[:, :], ALU.pow).then_inc(rstd3, 1)

            def body(g, b, front, lead):
                s = NB * g + b
                if front:
                    for m in (1, 3, 5):
                        h_rest(s + 1, m)
                rstd_out(s)
                if lead:
                    rstd_lead(s + 2)
                rstd_x1(b, s)
                if front:
                    v_rest(1 - b, s + 1)
                if lead:
                    residual(g + 1, b, False)

            pool.wait_ge(consts, 3)
            rstd_lead(0)
            nc.gpsimd.affine_select(out=tril[:, :], in_=tril[:, :], compare_op=ALU.is_ge, fill=0.0, base=0,
                                    pattern=[[1, P]], channel_multiplier=-1).then_inc(consts, 1)
            pool.wait_ge(small_in, 16 * 8)
            residual(0, 0, True)
            rstd_lead(1)
            residual(0, 1, True)
            for m in (1, 3, 5):
                h_rest(0, m)
            v_rest(0, 0)
            with pool.Fori(0, STEPS // NB - 1) as g:
                for b in range(NB):
                    body(g, b, True, True)

            nc.gpsimd.memset(ones[:, :], 1.0).then_inc(rconst, 1)
            nc.gpsimd.memset(keep8[:, :], 1.0)
            nc.gpsimd.memset(keep[:, :, :], 1.0).then_inc(rconst, 1)
            pool.wait_ge(rconst, 3)
            nc.gpsimd.memset(keep[:, :, 0:1], 0.0).then_inc(rconst, 1)
            nc.gpsimd.affine_select(out=lower[:, :], in_=ones[:, :], compare_op=ALU.is_gt, fill=0.0, base=0,
                                    pattern=[[1, P]], channel_multiplier=-1).then_inc(rconst, 1)
            exact = dict(allow_small_or_imprecise_dtypes=True)
            nc.gpsimd.iota(revt[:, :, :], [[-1, NT], [0, NJ]], base=NT, channel_multiplier=0, **exact)
            nc.gpsimd.iota(blk_edge[:, :, :], [[0, NT], [P, NJ]], base=0, channel_multiplier=0, **exact
                           ).then_inc(rconst, 1)
            nc.gpsimd.iota(edges[:, :, :], [[0, NJ], [P, NBLK + 1]], base=0, channel_multiplier=0, **exact
                           ).then_inc(rconst, 1)
            nc.gpsimd.iota(kcol[:, :, :], [[1, NBLK], [0, NT]], base=0, channel_multiplier=0, **exact)
            nc.gpsimd.iota(lane[:, :], [[1, P]], base=0, channel_multiplier=0, **exact)
            nc.gpsimd.iota(posn[:, :], [[P, NJ]], base=1, channel_multiplier=1, **exact).then_inc(rconst, 1)

            body(STEPS // NB - 1, 0, True, False)
            body(STEPS // NB - 1, 1, False, False)

            def gather(n, p, first):
                if not first:
                    pool.wait_ge(gidx_done, n - 1)
                    alone(pool, gate_pool)
                pool.indirect_dma_start(out=grow[p], out_offset=None, in_=scratch,
                                        in_offset=bass.IndirectOffsetOnAxis(
                                            ap=idx_i[:, n:n + 1] if first else gidx[p][:, :], axis=0)).then_inc(got[p], 16)

            def scatter(n, p):
                pool.wait_ge(y_done, n + 1)
                alone(pool, gate_pool)
                for b in range(NB):
                    pool.indirect_dma_start(out=out_rows, out_offset=bass.IndirectOffsetOnAxis(
                                                ap=sidx[p][:, b:b + 1], axis=0),
                                            in_=yb[p][:, b, :], in_offset=None, bounds_check=NB * T - 1,
                                            oob_is_err=False).then_inc(sent[p], 16)

            pool.wait_ge(rv, 49 + 4)
            for b in range(NB):
                pool.wait_ge(x1_out[b], 16 * STEPS // NB)
            gather(0, 0, True)
            gather(1, 1, True)
            gather(2, 0, False)
            with pool.Fori(0, (NBLK - 3) // 2) as i:
                scatter(2 * i, 0)
                gather(2 * i + 3, 1, False)
                scatter(2 * i + 1, 1)
                gather(2 * i + 4, 0, False)
            scatter(NBLK - 3, 0)
            scatter(NBLK - 2, 1)
            scatter(NBLK - 1, 0)
            pool.wait_ge(sent[0], 32 * ((NBLK + 1) // 2))
            pool.wait_ge(sent[1], 32 * (NBLK // 2))


def position_table(seq, dim):
    import math
    import numpy as np
    pos = np.arange(seq, dtype=np.float32)[:, None]
    step = np.arange(0, dim, 2, dtype=np.float32) * np.float32(-math.log(10000.0) / dim)
    angle = (pos * np.exp(step.astype(np.float64)).astype(np.float32)).astype(np.float64)
    table = np.zeros((seq, dim), dtype=np.float32)
    table[:, 0::2] = np.sin(angle)
    table[:, 1::2] = np.cos(angle)
    return np.ascontiguousarray(table.T)


_INS = ['L0_attn_x', 'L0_attn_W1q', 'L0_attn_b1q', 'L0_attn_W2q', 'L0_attn_b2q', 'L0_attn_W1k', 'L0_attn_b1k',
        'L0_attn_W2k', 'L0_attn_b2k', 'L0_attn_W1v', 'L0_attn_b1v', 'L0_attn_W2v', 'L0_attn_b2v', 'L0_attn_ln_w',
        'L0_attn_ln_b', 'L0_ffn_tile_sigs', 'L0_ffn_W', 'L0_ffn_b']


def kernel(**inputs):
    import numpy as _np
    import concourse.bacc as _bacc
    from concourse import mybir as _mybir
    from concourse.bass_utils import run_bass_kernel_spmd as _run

    nc = _bacc.Bacc("TRN2", target_bir_lowering=False, num_devices=1)
    arrays, ap = {}, {}
    for name in _INS:
        a = _np.ascontiguousarray(inputs[name])
        arrays[f"in_{name}_dram"] = a
        ap[name] = nc.dram_tensor(f"in_{name}_dram", a.shape, _mybir.dt.from_np(a.dtype), kind="ExternalInput").ap()
    arrays["position_table"] = position_table(T, DP)
    pe = nc.dram_tensor("position_table", (DP, T), F32, kind="ExternalInput").ap()
    out = nc.dram_tensor("out_0_dram", (NB, T, C), F32, kind="ExternalOutput").ap()
    mk_seq_kernel(nc, ap['L0_attn_x'], [ap[f'L0_attn_W1{n}'] for n in 'qkv'], [ap[f'L0_attn_b1{n}'] for n in 'qkv'],
                  [ap[f'L0_attn_W2{n}'] for n in 'qkv'], [ap[f'L0_attn_b2{n}'] for n in 'qkv'],
                  ap['L0_attn_ln_w'], ap['L0_attn_ln_b'], ap['L0_ffn_tile_sigs'], ap['L0_ffn_W'], ap['L0_ffn_b'],
                  pe, out)
    r = _run(nc, [arrays], core_ids=[0])
    return r.results[0]["out_0_dram"]
```

```python
from contextlib import ExitStack

import concourse.bass as bass
from concourse import mybir

F32 = mybir.dt.float32
F32R = mybir.dt.float32r
I32 = mybir.dt.int32
ALU = mybir.AluOpType
ACT = mybir.ActivationFunctionType
AX_X = mybir.AxisListType.X

P = 128
NB = 2
T = 2048
C = 256
KC = C // P
GT = 512
CH = GT // P
STEPS = NB * T // GT
NT = 8
DP = 32
EPS = 1e-5
INV_SCALE = float((C * 512) ** -0.5)
NJ = T // P
ROW = C + 2
NBLK = (T + NT * (P - 1)) // P
FAR = 8192
FILLS = 16
SPLIT = ((0, 0), (0, 1), (1, 0))
Q, K, V = range(3)
RB = 4
ROUTED = 53


def mk_seq_kernel(nc, x, w1, b1, w2, b2, ln_w, ln_b, sigs, ffn_w, ffn_b, pe, out):
    scratch = nc.dram_tensor("x1_rows", [T, NB * ROW], F32, kind="Internal").ap()
    rows_sbp = scratch.rearrange("(g c p) (b d) -> g b p c d", p=P, c=CH, b=NB)
    x_gbp = x.rearrange("b (g c p) d -> g b p c d", p=P, c=CH)
    out_rows = out.rearrange("b s d -> (b s) d")

    with ExitStack() as ctx:
        def sb(name, shape, dt=F32):
            return ctx.enter_context(nc.sbuf_tensor(name, shape, dt))

        def sem(name):
            return ctx.enter_context(nc.semaphore(name))

        w_stage = sb("w_stage", [P, 6, KC, C])
        w_all = sb("w_all", [P, NT, 2, KC * C], F32R)
        w_sp = w_all[:, 0:6].rearrange("p m a (k c) -> p m a k c", k=KC)
        wf_sp = w_all
        b1c = sb("b1c", [P, 3, KC])
        b2c = sb("b2c", [P, 2, KC])
        b2v_row = sb("b2v_row", [P, C])
        lnw_row = sb("lnw_row", [P, C])
        lnb_row = sb("lnb_row", [P, C])
        ident = sb("ident", [P, P])
        tril = sb("tril", [P, P])
        half = sb("half", [P, CH])
        xt = [sb(f"xt{b}", [P, CH, C]) for b in range(NB)]
        xres = [sb(f"xres{b}", [P, CH, ROW]) for b in range(NB)]
        xn = sb("xn", [P, CH, C])
        st1 = sb("st1", [P, CH, 6])
        mv1 = sb("mv1", [P, CH, 2])
        ve1 = sb("ve1", [P, CH])
        rs1 = sb("rs1", [P, CH])
        xnT = sb("xnT", [P, 2, KC, GT], F32R)
        h32 = sb("h32", [P, 6, GT])
        hT = sb("hT", [P, 6, 2, GT], F32R)
        qT = [sb(f"qT{b}", [P, 2, KC, GT], F32R) for b in range(NB)]
        k32 = sb("k32", [P, KC, GT])
        kT = sb("kT", [P, 2, KC, GT], F32R)
        ktok = [sb(f"ktok{b}", [P, 2, CH, C], F32R) for b in range(NB)]
        v32 = sb("v32", [P, CH, C])
        vtok = [sb(f"vtok{b}", [P, 2, CH, C], F32R) for b in range(NB)]
        sc32 = sb("sc32", [P, GT])
        scT = sb("scT", [P, 2, GT], F32R)
        state = [sb(f"state{b}", [P, 2, KC * C], F32R) for b in range(NB)]
        cen = sb("cen", [P, CH, C])
        st2 = sb("st2", [P, CH, 6])
        mv2 = sb("mv2", [P, CH, 2])
        ve2 = sb("ve2", [P, CH])
        rs2 = sb("rs2", [P, CH])
        st3 = sb("st3", [P, CH, 6])
        mv3 = sb("mv3", [P, CH, 2])
        ve3 = sb("ve3", [P, CH])
        nm3 = sb("nm3", [P, CH])

        ring = [ctx.enter_context(nc.psum_tensor(f"ring{i}", [P, 512], F32)) for i in range(3)]
        sc_ps = ctx.enter_context(nc.psum_tensor("sc_ps", [P, 512], F32))
        o_ps = [ctx.enter_context(nc.psum_tensor(f"o_ps{i}", [P, 512], F32)) for i in range(2)]
        s_ps = [ctx.enter_context(nc.psum_tensor(f"s_ps{b}", [P, 512], F32)) for b in range(NB)]

        x_in = [sem(f"x_in{b}") for b in range(NB)]
        w_in = [sem(f"w_in{i}") for i in range(6)]
        small_in = sem("small_in")
        ffn_in = sem("ffn_in")
        route_in = sem("route_in")
        consts = sem("consts")
        zeroed = sem("zeroed")
        w_scaled = sem("w_scaled")
        w_hi = sem("w_hi")
        w_lo = sem("w_lo")
        stat1 = sem("stat1")
        aggr1 = sem("aggr1")
        var1 = sem("var1")
        rstd1 = sem("rstd1")
        xn_done = sem("xn_done")
        res_done = sem("res_done")
        fill = sem("fill")
        xnT_hi = sem("xnT_hi")
        xnT_lo = sem("xnT_lo")
        gelu = sem("gelu")
        h_hi = sem("h_hi")
        h_lo_dve = sem("h_lo_dve")
        h_lo_pool = sem("h_lo_pool")
        q_hi = sem("q_hi")
        q_lo = sem("q_lo")
        k_full = sem("k_full")
        k_hi = sem("k_hi")
        k_lo = sem("k_lo")
        v_sum = sem("v_sum")
        v_hi = sem("v_hi")
        v_lo = sem("v_lo")
        ktok_hi = sem("ktok_hi")
        ktok_lo = sem("ktok_lo")
        scores = sem("scores")
        sc_mask = sem("sc_mask")
        sc_hi = sem("sc_hi")
        sc_lo = sem("sc_lo")
        o_ready = sem("o_ready")
        s_ready = sem("s_ready")
        s_hi = sem("s_hi")
        s_lo = sem("s_lo")
        o_stat = sem("o_stat")
        o_aggr = sem("o_aggr")
        o_cen = sem("o_cen")
        var2 = sem("var2")
        rstd2 = sem("rstd2")
        x1_made = sem("x1_made")
        stat3 = sem("stat3")
        aggr3 = sem("aggr3")
        var3 = sem("var3")
        rstd3 = sem("rstd3")
        shift3 = sem("shift3")
        x1_out = [sem(f"x1_out{b}") for b in range(NB)]

        sgn = sb("sgn", [DP, 3, NT])
        sig_in = sb("sig_in", [DP, NT])
        peT = [xt[i][0:DP, :, :].rearrange("p c d -> p (c d)") for i in range(2)]
        h_flat = h32[:, :, :].rearrange("p m n -> p (m n)")
        carved = [0]

        def carve(*dims, parts=P):
            n, at = 1, carved[0]
            for d in dims:
                n *= d
            carved[0] += n
            names = "abc"[:len(dims)]
            return h_flat[0:parts, at:at + n].rearrange(f"p ({' '.join(names)}) -> p {' '.join(names)}",
                                                        **dict(zip(names, dims)))

        rsc = carve(NT, NJ)
        rmax = sb("rmax", [P, NJ])
        req = carve(NT, NJ)
        rcand = carve(NT, NJ)
        rbest = sb("rbest", [P, NJ])
        onehot = carve(NT, NJ)
        lower = sb("lower", [P, P])
        ones = sb("ones", [P, P])
        revt = sb("revt", [P, NT, NJ])
        keep = sb("keep", [P, NT, NJ])
        tot = carve(NT, NJ)
        incl = carve(NT, NJ)
        zed = carve(NT, NJ)
        slot_t = carve(NT, NJ)
        slot = sb("slot", [P, NJ])
        blk_edge = sb("blk_edge", [P, NT, NJ])
        blk_gt = carve(NT, NJ)
        blks = sb("blks", [P, NT])
        ends = sb("ends", [P, NT])
        keep8 = sb("keep8", [P, NT])
        starts = sb("starts", [P, NT])
        k_flat = k32[:, :, :].rearrange("p k n -> p (k n)")
        kcol = k_flat[0:1, 512:512 + NBLK * NT].rearrange("p (k t) -> p k t", k=NBLK)
        kge = carve(NBLK, NT, parts=1)
        tile_f = sb("tile_f", [1, 2, NBLK])
        tile_i = sb("tile_i", [1, NBLK], I32)
        edges = k_flat[:, 0:NJ * (NBLK + 1)].rearrange("p (j k) -> p j k", j=NJ)
        above = carve(NJ, NBLK + 1)
        inblk = carve(NJ, NBLK)
        posn = sb("posn", [P, NJ])
        poscol = carve(NJ, NBLK)
        nblk = sb("nblk", [P, NJ])
        rest = sb("rest", [P, NJ])
        lane = sb("lane", [P, P])
        lane_oh = [(xn if j < CH * KC else v32)[:, j // KC % CH, j % KC * P:j % KC * P + P] for j in range(NJ)]
        idx_f = sb("idx_f", [P, 5, NBLK])
        idx_i = sb("idx_i", [P, 3 * NBLK], I32)
        gidx = [sb(f"gidx{i}", [P, 1], I32) for i in range(RB)]
        sidx = [sb(f"sidx{i}", [P, NB], I32) for i in range(RB)]
        ffn_stage = w_stage[:, :, :, :].rearrange("p a k c -> p (a k c)")[:, 0:4 * 512].rearrange(
            "p (t k c) -> p t k c", t=4, k=KC)
        bias_rows = sb("bias_rows", [P, NT, C])
        x_flat = [a.rearrange("p c d -> p (c d)") for a in (xt[0][:, :, :], xt[1][:, :, :], cen[:, :, :])]
        w_flat = w_stage[:, :, :, :].rearrange("p a k c -> p (a k c)")
        grow = [a[:, 0:NB * ROW] for a in x_flat] + [w_flat[:, 4 * 512:4 * 512 + NB * ROW]]
        resb = [h32[:, i, :].rearrange("p (b d) -> p b d", b=NB) for i in range(RB)]
        yb = [w_flat[:, i * 512:i * 512 + 512].rearrange("p (b d) -> p b d", b=NB) for i in range(RB)]
        xnb = [a[:, i:i + NB] for a in (xn, v32) for i in (0, NB)]
        xbT = [hT[:, i] for i in range(RB)]
        t_bank = ring + [s_ps[0]]
        y_bank = o_ps + [sc_ps, s_ps[1]]

        rconst = sem("rconst")
        rv = sem("rv")
        rp = sem("rp")
        wf_t = sem("wf_t")
        wf_hi = sem("wf_hi")
        wf_lo = sem("wf_lo")
        got = [sem(f"got{i}") for i in range(RB)]
        sent = [sem(f"sent{i}") for i in range(RB)]
        xnb_done = sem("xnb_done")
        resb_done = sem("resb_done")
        xb_t = sem("xb_t")
        xb_hi = sem("xb_hi")
        xb_lo = sem("xb_lo")
        y_ps = sem("y_ps")
        y_done = sem("y_done")

        gate_dve = sem("gate_dve")
        gate_pool = sem("gate_pool")

        block = ctx.enter_context(nc.Block())

        def alone(eng, gate):
            eng.sem_inc(gate, 1)

        def cols(c):
            return slice(c * P, (c + 1) * P)

        def over_slots(eng, one_slot):
            head = RB + 1
            loops = (NBLK - RB - head) // RB
            for k in range(head):
                one_slot(k // RB, k % RB, True)
            with eng.Fori(0, loops) as i:
                for k in range(head, head + RB):
                    one_slot(i + k // RB, k % RB, False)
            for k in range(head + RB * loops, NBLK + 1):
                one_slot(k // RB, k % RB, True)

        @block.sync
        def _(sp):
            def load_x(g, b):
                sp.dma_start(xt[b][:, :, :], x_gbp[bass.ds(g, 1), b].rearrange("g p c d -> p (g c) d")
                             ).then_inc(x_in[b], 16)

            def store(g, b):
                sp.wait_ge(shift3, NB * g + b + 1)
                sp.dma_start(rows_sbp[bass.ds(g, 1), b].rearrange("g p c d -> p (g c) d"), xres[b][:, :, :]
                             ).then_inc(x1_out[b], 16)

            load_x(0, 0)
            for i, w in enumerate((w1[Q], w1[K], w1[V], w2[Q], w2[K], w2[V])):
                sp.dma_start(w_stage[:, i, :, :], w.rearrange("(k p) n -> p k n", p=P)).then_inc(w_in[i], 16)
                if i == 0:
                    load_x(0, 1)
            sp.wait_ge(xn_done, 1)
            sp.wait_ge(res_done, 1)
            load_x(1, 0)
            sp.dma_start(bias_rows[:, :, :], ffn_b.partition_broadcast(P)).then_inc(route_in, 16)
            sp.dma_start(sig_in[:, :], sigs.rearrange("t d -> d t"), allow_slow_non_contiguous=True).then_inc(route_in, 16)

            def body(g, b, front, lead):
                if lead:
                    sp.wait_ge(xn_done, NB * g + b + 2)
                    sp.wait_ge(res_done, NB * g + b + 2)
                    load_x(g + 1 + b, 1 - b)
                store(g, b)

            with sp.Fori(0, STEPS // NB - 2) as g:
                for b in range(NB):
                    body(g, b, True, True)
            body(STEPS // NB - 2, 0, True, True)
            body(STEPS // NB - 2, 1, True, False)
            ffn_v = ffn_w.rearrange("t (k p) d -> p t k d", p=P)
            sp.wait_ge(w_lo, 6)
            sp.dma_start(ffn_stage, ffn_v[:, 0:4]).then_inc(ffn_in, 16)
            sp.wait_ge(xn_done, STEPS)
            sp.wait_ge(res_done, STEPS)
            for i in range(2):
                sp.dma_start(peT[i], pe[:, i * T // 2:(i + 1) * T // 2]).then_inc(route_in, 16)
            body(STEPS // NB - 1, 0, True, False)
            sp.wait_ge(wf_t, 4)
            sp.dma_start(ffn_stage, ffn_v[:, 4:8]).then_inc(ffn_in, 16)
            body(STEPS // NB - 1, 1, False, False)

        @block.tensor
        def _(te):
            def mm3(o, lhs, rhs, start=True, stop=True, check=False):
                n = len(lhs)
                for k in range(n):
                    for i, (a, c) in enumerate(SPLIT):
                        last = te.matmul(o, lhs[k][a], rhs[k][c], start=start and k == 0 and i == 0,
                                         stop=stop and k == n - 1 and i == 2, skip_group_check=check)
                return last

            def wpair(m, k, n0, n1):
                return [w_sp[:, m, a, k, n0:n1] for a in range(2)]

            def front_transposes(s, first):
                te.wait_ge(xn_done, s + 1)
                for k in range(KC):
                    if not first:
                        te.wait_ge(v_sum if k else ktok_lo, 2 * s)
                    for c in range(CH):
                        last = te.transpose(ring[k][:, cols(c)], xn[:, c, cols(k)], ident[:, :])
                    last.then_inc(fill, 1)

            def front_h(s, ms, first):
                for m in ms:
                    if m >= 3:
                        te.wait_ge(gelu, 6 * s + m - 2)
                    if first and m % 2 == 0:
                        te.wait_ge(w_lo, m // 2 + 1)
                    for k in range(KC):
                        if m == 0:
                            te.wait_ge(xnT_lo, 2 * s + 1 + k)
                        last = mm3(ring[(2 + m) % 3][:, :], [wpair(m // 2, k, m % 2 * P, m % 2 * P + P)],
                                   [[xnT[:, a, k, :] for a in range(2)]], start=k == 0, stop=k == KC - 1)
                    last.then_inc(fill, 1)

            def front_qk(s, which, first):
                te.wait_ge(h_lo_dve, 3 * s + which + 1)
                te.wait_ge(h_lo_pool, 3 * s + which + 1)
                if first:
                    te.wait_ge(w_lo, 4 + which)
                for j in (2 * which, 2 * which + 1):
                    if j < 3:
                        te.wait_ge(gelu, 6 * s + 4 + j)
                    else:
                        te.wait_ge(q_lo, 2 * s + 1)
                    mm3(ring[(8 + j) % 3][:, :], [wpair(3 + which, k, j % 2 * P, j % 2 * P + P) for k in range(KC)],
                        [[hT[:, 2 * which + k, a, :] for a in range(2)] for k in range(KC)]).then_inc(fill, 1)

            def front_v(s, first):
                te.wait_ge(h_lo_dve, 3 * s + 3)
                te.wait_ge(h_lo_pool, 3 * s + 3)
                if first:
                    te.wait_ge(w_lo, 6)
                for j in range(2):
                    if j == 0:
                        te.wait_ge(q_lo, 2 * s + 2)
                    else:
                        te.wait_ge(k_full, 2 * s + 1)
                    for c in (2 * j, 2 * j + 1):
                        last = mm3(ring[j][:, c % 2 * C:c % 2 * C + C],
                                   [[hT[:, 4 + k, a, cols(c)] for a in range(2)] for k in range(KC)],
                                   [wpair(5, k, 0, C) for k in range(KC)])
                    last.then_inc(fill, 1)

            def front_scores(b, s, first):
                te.wait_ge(q_lo, 2 * s + 2)
                te.wait_ge(k_lo, 2 * s + 2)
                if not first:
                    te.wait_ge(sc_mask, s)
                for c in range(CH):
                    last = mm3(sc_ps[:, cols(c)], [[kT[:, a, k, cols(c)] for a in range(2)] for k in range(KC)],
                               [[qT[b][:, a, k, cols(c)] for a in range(2)] for k in range(KC)])
                last.then_inc(scores, 1)

            def front_ktok(s):
                for n in range(2):
                    if n == 0:
                        te.wait_ge(k_full, 2 * s + 2)
                    else:
                        te.wait_ge(v_sum, 2 * s + 1)
                    for i in range(4):
                        last = te.transpose(ring[(14 + n) % 3][:, cols(i)], k32[:, i % 2, cols(2 * n + i // 2)],
                                            ident[:, :])
                    last.then_inc(fill, 1)

            def back_chunk(b, s, c):
                te.wait_ge(s_lo, 4 * s + c + 1)
                te.wait_ge(o_cen, 4 * s + c + 1)
                o = o_ps[c % 2][:, 0:C]
                mm3(o, [[qT[b][:, a, k, cols(c)] for a in range(2)] for k in range(KC)],
                    [[state[b][:, a, k * C:k * C + C] for a in range(2)] for k in range(KC)], stop=False)
                if c == 0:
                    te.wait_ge(v_lo, 2 * s + 2)
                    te.wait_ge(ktok_lo, 2 * s + 2)
                vs = [vtok[b][:, a, c, :] for a in range(2)]
                for k in range(KC):
                    last = mm3(s_ps[b][:, k * C:k * C + C], [[ktok[b][:, a, c, cols(k)] for a in range(2)]], [vs],
                               start=False, check=True)
                last.then_inc(s_ready, 1)
                if c == 0:
                    te.wait_ge(sc_lo, s + 1)
                mm3(o, [[scT[:, a, cols(c)] for a in range(2)]], [vs], start=False).then_inc(o_ready, 1)

            def body(g, b, front, lead, fillers=None):
                s = NB * g + b
                if front:
                    front_transposes(s + 1, False)
                back_chunk(b, s, 0)
                for c in range(1, CH):
                    if front:
                        front_h(s + 1, (2 * c - 2, 2 * c - 1), False)
                    elif fillers:
                        fillers(c - 1)
                    back_chunk(b, s, c)
                if front:
                    front_qk(s + 1, 0, False)
                    front_qk(s + 1, 1, False)
                    front_v(s + 1, False)
                    front_ktok(s + 1)
                    front_scores(1 - b, s + 1, False)

            te.wait_ge(consts, 2)
            front_transposes(0, True)
            te.wait_ge(zeroed, 2)
            front_h(0, range(6), True)
            front_qk(0, 0, True)
            front_qk(0, 1, True)
            front_v(0, True)
            front_ktok(0)
            front_scores(0, 0, True)
            with te.Fori(0, STEPS // NB - 1) as g:
                for b in range(NB):
                    body(g, b, True, True)
            body(STEPS // NB - 1, 0, True, False)

            def tile_weights(t):
                te.wait_ge(ffn_in, 16 * (t // 4 + 1))
                if t < 3:
                    te.wait_ge(ktok_lo, 2 * STEPS)
                else:
                    te.wait_ge(wf_lo, t - 2)
                for k in range(KC):
                    for o in range(KC):
                        last = te.transpose(ring[t % 3][:, k * C + o * P:k * C + o * P + P],
                                            ffn_stage[:, t % 4, o, cols(k)], ident[:, :])
                last.then_inc(wf_t, 1)

            def route_scores():
                te.wait_ge(rv, 3)
                te.wait_ge(route_in, 64)
                te.wait_ge(sc_mask, STEPS)
                for j in range(NJ):
                    last = te.matmul(sc_ps[:, j * NT:j * NT + NT], peT[j // 8][:, cols(j % 8)], sgn[:, 2, :],
                                     start=True, stop=True)
                last.then_inc(rp, 1)

            def route_counts():
                te.wait_ge(rv, 9)
                te.wait_ge(rconst, 7)
                oh = onehot[:, :, :].rearrange("p t j -> p (t j)")
                te.matmul(sc_ps[:, 128:256], lower[:, :], oh, start=True, stop=True)
                te.matmul(sc_ps[:, 256:384], ones[:, :], oh, start=True, stop=True).then_inc(rp, 1)

            def route_invert():
                te.wait_ge(rv, 26)
                for j in range(NJ):
                    te.wait_ge(rv, 27 + j)
                    last = te.matmul(sc_ps[:, 0:NBLK], lane_oh[j], poscol[:, j, :], start=(j == 0),
                                     stop=(j == NJ - 1))
                last.then_inc(rp, 1)

            def fillers(n):
                if n == 0:
                    route_scores()
                    for t in range(0, 2):
                        tile_weights(t)
                if n == 1:
                    route_counts()
                    for t in range(2, 4):
                        tile_weights(t)
                if n == 2:
                    route_invert()

            body(STEPS // NB - 1, 1, False, False, fillers)
            for t in range(4, NT):
                tile_weights(t)

            def block_transposes(n, p, first):
                te.wait_ge(xnb_done, n + 1)
                if not first:
                    te.wait_ge(xb_lo, n - RB + 1)
                for b in range(NB):
                    for k in range(KC):
                        last = te.transpose(t_bank[p][:, b * C + k * P:b * C + k * P + P], xnb[p][:, b, cols(k)],
                                            ident[:, :])
                last.then_inc(xb_t, 1)

            def block_products(n, p, first):
                t = te.value_load(tile_i[0:1, bass.ds(n, 1)], min_val=0, max_val=NT - 1)
                te.wait_ge(xb_lo, n + 1)
                if not first:
                    te.wait_ge(y_done, n - RB + 1)
                for b in range(NB):
                    last = mm3(y_bank[p][:, b * C:b * C + C],
                               [[xbT[p][:, a, b * C + k * P:b * C + k * P + P] for a in range(2)] for k in range(KC)],
                               [[wf_sp[:, bass.ds(t, 1), a, k * C:k * C + C].rearrange("p t c -> p (t c)")
                                 for a in range(2)] for k in range(KC)])
                last.then_inc(y_ps, 1)

            te.wait_ge(wf_lo, NT)
            te.wait_ge(o_cen, 4 * STEPS + 2)
            te.wait_ge(s_lo, 4 * STEPS + 1)
            te.wait_ge(rv, ROUTED)

            def one_slot(turn, j, edge):
                n = RB * turn + j
                if not edge or n < NBLK:
                    block_transposes(n, j, edge and n < RB)
                if not edge or n > 0:
                    block_products(n - 1, (j - 1) % RB, edge and n - 1 < RB)

            over_slots(te, one_slot)

        @block.scalar
        def _(act):
            for i in range(3):
                act.dma_start(b1c[:, i, :], b1[i].rearrange("(k p) -> p k", p=P),
                              allow_slow_non_contiguous=True).then_inc(small_in, 16)
            for i in range(2):
                act.dma_start(b2c[:, i, :], b2[i].rearrange("(k p) -> p k", p=P),
                              allow_slow_non_contiguous=True).then_inc(small_in, 16)
            act.dma_start(lnb_row[:, :], ln_b.partition_broadcast(P)).then_inc(small_in, 16)
            act.dma_start(lnw_row[:, :], ln_w.partition_broadcast(P)).then_inc(small_in, 16)
            act.dma_start(b2v_row[:, :], b2[V].partition_broadcast(P)).then_inc(small_in, 16)

            def xnT_rounded(s):
                for k in range(KC):
                    act.wait_ge(fill, FILLS * s + 1 + k)
                    nc.scalar.copy(xnT[:, 0, k, :], ring[k][:, :]).then_inc(xnT_hi, 1)

            def gelus(s, ms):
                for m in ms:
                    act.wait_ge(fill, FILLS * s + 3 + m)
                    nc.scalar.activation(h32[:, m, :], ring[(2 + m) % 3][:, :], ACT.Gelu,
                                         bias=b1c[:, m // 2, m % 2:m % 2 + 1]).then_inc(gelu, 1)

            def h_rounded(s, m):
                act.wait_ge(gelu, 6 * s + m + 1)
                nc.scalar.copy(hT[:, m, 0, :], h32[:, m, :]).then_inc(h_hi, 1)

            def q_rounded(b, s):
                for j in range(2):
                    act.wait_ge(fill, FILLS * s + 9 + j)
                    nc.scalar.activation(qT[b][:, 0, j, :], ring[(8 + j) % 3][:, :], ACT.Identity,
                                         bias=b2c[:, Q, j:j + 1]).then_inc(q_hi, 1)

            def k_rounded(s):
                for j in range(2):
                    act.wait_ge(fill, FILLS * s + 11 + j)
                    nc.scalar.activation(k32[:, j, :], ring[(10 + j) % 3][:, :], ACT.Identity,
                                         bias=b2c[:, K, j:j + 1]).then_inc(k_full, 1)
                    act.wait_ge(k_full, 2 * s + 1 + j)
                    nc.scalar.copy(kT[:, 0, j, :], k32[:, j, :]).then_inc(k_hi, 1)

            def v_rounded(b, s):
                for j in range(2):
                    act.wait_ge(v_sum, 2 * s + 1 + j)
                    nc.scalar.copy(vtok[b][:, 0, 2 * j:2 * j + 2, :], v32[:, 2 * j:2 * j + 2, :]).then_inc(v_hi, 1)

            def scores_rounded(s):
                act.wait_ge(sc_mask, s + 1)
                nc.scalar.copy(scT[:, 0, :], sc32[:, :]).then_inc(sc_hi, 1)

            def ktok_rounded(b, s):
                for n in range(2):
                    act.wait_ge(fill, FILLS * s + 15 + n)
                    nc.scalar.copy(ktok[b][:, 0, 2 * n:2 * n + 2, :],
                                   ring[(14 + n) % 3][:, :].rearrange("p (c d) -> p c d", c=2)
                                   ).then_inc(ktok_hi, 1)

            def state_rounded(b, s, c):
                act.wait_ge(s_ready, 4 * s + c + 1)
                nc.scalar.copy(state[b][:, 0, :], s_ps[b][:, :]).then_inc(s_hi, 1)

            def tile_rounded(ts):
                for t in ts:
                    act.wait_ge(wf_t, t + 1)
                    nc.scalar.copy(wf_sp[:, t, 0, :], ring[t % 3][:, :]).then_inc(wf_hi, 1)

            def body(g, b, front, lead, fillers=None):
                s = NB * g + b
                if front:
                    xnT_rounded(s + 1)
                state_rounded(b, s, 0)
                for c in range(1, CH):
                    if front:
                        for m in (2 * c - 2, 2 * c - 1):
                            gelus(s + 1, (m,))
                            h_rounded(s + 1, m)
                    elif fillers:
                        fillers(c - 1)
                    state_rounded(b, s, c)
                if front:
                    q_rounded(1 - b, s + 1)
                    k_rounded(s + 1)
                    v_rounded(1 - b, s + 1)
                    ktok_rounded(1 - b, s + 1)
                    scores_rounded(s + 1)

            for i in range(6):
                if i < 3:
                    act.wait_ge(w_in[i], 16)
                else:
                    act.wait_ge(w_scaled, 1)
                    act.wait_ge(w_in[i], 16)
                nc.scalar.copy(w_sp[:, i, 0, :, :], w_stage[:, i, :, :]).then_inc(w_hi, 1)
                if i == 1:
                    xnT_rounded(0)
            act.wait_ge(small_in, 16 * 8)
            for m in range(6):
                gelus(0, (m,))
                h_rounded(0, m)
            q_rounded(0, 0)
            k_rounded(0)
            v_rounded(0, 0)
            ktok_rounded(0, 0)
            scores_rounded(0)
            with act.Fori(0, STEPS // NB - 1) as g:
                for b in range(NB):
                    body(g, b, True, True)
            body(STEPS // NB - 1, 0, True, False)

            def fillers(n):
                if n < 2:
                    tile_rounded((2 * n, 2 * n + 1))

            body(STEPS // NB - 1, 1, False, False, fillers)
            tile_rounded(range(4, NT))

            def block_norm(turn, p, first):
                n = RB * turn + p
                act.wait_ge(got[p], 16 * turn + 16)
                if not first:
                    act.wait_ge(xb_t, n - RB + 1)
                for b in range(NB):
                    r = grow[p][:, b * ROW:(b + 1) * ROW]
                    last = nc.scalar.activation(xnb[p][:, b, :], r[:, 0:C], ACT.Identity, bias=r[:, C:C + 1],
                                                scale=r[:, C + 1:C + 2])
                last.then_inc(xnb_done, 1)

            def block_rounded(n, p):
                act.wait_ge(xb_t, n + 1)
                nc.scalar.copy(xbT[p][:, 0, :], t_bank[p][:, :]).then_inc(xb_hi, 1)

            act.wait_ge(rp, 3)
            block_norm(0, 0, True)

            def one_slot(turn, j, edge):
                n = RB * turn + j
                if not edge or n < NBLK:
                    block_rounded(n, j)
                if not edge or n + 1 < NBLK:
                    block_norm(turn + (j + 1) // RB, (j + 1) % RB, edge and n + 1 < RB)

            over_slots(act, one_slot)

        @block.vector
        def _(dve):
            def lead_stat(g, b, c):
                if c == 0:
                    dve.wait_ge(x_in[b], 16 * (g + 1))
                nc.vector.bn_stats(st1[:, c, :], xt[b][:, c, :]).then_inc(stat1, 1)

            def lead_var(g, b):
                s = NB * g + b
                dve.wait_ge(stat1, CH * s + CH)
                alone(dve, gate_dve)
                for c in range(CH):
                    last = nc.vector.bn_aggr(mv1[:, c, :], st1[:, c, :])
                last.then_inc(aggr1, 1)
                dve.wait_ge(aggr1, s + 1)
                nc.vector.tensor_scalar(ve1[:, :], mv1[:, :, 1], EPS, None, ALU.add).then_inc(var1, 1)

            def lead_norm(g, b, first):
                s = NB * g + b
                dve.wait_ge(rstd1, s + 1)
                if not first:
                    dve.wait_ge(fill, FILLS * (s - 1) + 2)
                for c in range(CH):
                    last = nc.vector.tensor_scalar(xn[:, c, :], xt[b][:, c, :], mv1[:, c, 0:1], rs1[:, c:c + 1],
                                                   ALU.subtract, ALU.mult)
                last.then_inc(xn_done, 1)

            def xnT_rest(s):
                for k in range(KC):
                    dve.wait_ge(xnT_hi, 2 * s + 1 + k)
                    nc.vector.tensor_tensor(xnT[:, 1, k, :], ring[k][:, :], xnT[:, 0, k, :].bitcast(F32),
                                            ALU.subtract).then_inc(xnT_lo, 1)

            def h_rest(s, m):
                dve.wait_ge(h_hi, 6 * s + m + 1)
                nc.vector.tensor_tensor(hT[:, m, 1, :], h32[:, m, :], hT[:, m, 0, :].bitcast(F32),
                                        ALU.subtract).then_inc(h_lo_dve, 1)

            def q_rest(b, s):
                for j in range(2):
                    dve.wait_ge(q_hi, 2 * s + 1 + j)
                    nc.vector.scalar_tensor_tensor(out=qT[b][:, 1, j, :], in0=ring[(8 + j) % 3][:, :],
                                                   scalar=b2c[:, Q, j:j + 1], in1=qT[b][:, 0, j, :].bitcast(F32),
                                                   op0=ALU.add, op1=ALU.subtract).then_inc(q_lo, 1)

            def k_rest(s):
                for j in range(2):
                    dve.wait_ge(k_hi, 2 * s + 1 + j)
                    nc.vector.tensor_tensor(kT[:, 1, j, :], k32[:, j, :], kT[:, 0, j, :].bitcast(F32),
                                            ALU.subtract).then_inc(k_lo, 1)

            def ktok_rest(b, s):
                for n in range(2):
                    dve.wait_ge(ktok_hi, 2 * s + 1 + n)
                    nc.vector.tensor_tensor(ktok[b][:, 1, 2 * n:2 * n + 2, :],
                                            ring[(14 + n) % 3][:, :].rearrange("p (c d) -> p c d", c=2),
                                            ktok[b][:, 0, 2 * n:2 * n + 2, :].bitcast(F32),
                                            ALU.subtract).then_inc(ktok_lo, 1)

            def v_biased(s, j):
                dve.wait_ge(fill, FILLS * s + 13 + j)
                nc.vector.tensor_tensor(v32[:, 2 * j:2 * j + 2, :], ring[j][:, :].rearrange("p (c d) -> p c d", c=2),
                                        b2v_row[:, :].unsqueeze(1).broadcast_to([P, 2, C]),
                                        ALU.add).then_inc(v_sum, 1)

            def scores_masked(s):
                dve.wait_ge(scores, s + 1)
                nc.vector.tensor_tensor(sc32[:, :].rearrange("p (c i) -> p c i", c=CH),
                                        sc_ps[:, :].rearrange("p (c i) -> p c i", c=CH),
                                        tril[:, :].unsqueeze(1).broadcast_to([P, CH, P]), ALU.mult).then_inc(sc_mask, 1)

            def scores_rest(s):
                dve.wait_ge(sc_hi, s + 1)
                nc.vector.tensor_tensor(scT[:, 1, :], sc32[:, :], scT[:, 0, :].bitcast(F32),
                                        ALU.subtract).then_inc(sc_lo, 1)

            def state_rest(b, s, c):
                dve.wait_ge(s_hi, 4 * s + c + 1)
                nc.vector.tensor_tensor(state[b][:, 1, :], s_ps[b][:, :], state[b][:, 0, :].bitcast(F32),
                                        ALU.subtract).then_inc(s_lo, 1)

            def out_centred(s, c):
                o = o_ps[c % 2][:, 0:C]
                dve.wait_ge(o_ready, 4 * s + c + 1)
                nc.vector.bn_stats(st2[:, c, :], o).then_inc(o_stat, 1)
                dve.wait_ge(o_stat, 4 * s + c + 1)
                alone(dve, gate_dve)
                nc.vector.bn_aggr(mv2[:, c, :], st2[:, c, :]).then_inc(o_aggr, 1)
                dve.wait_ge(o_aggr, 4 * s + c + 1)
                nc.vector.scalar_tensor_tensor(out=cen[:, c, :], in0=o, scalar=mv2[:, c, 0:1], in1=lnw_row[:, :],
                                               op0=ALU.subtract, op1=ALU.mult).then_inc(o_cen, 1)

            def out_var(s):
                nc.vector.tensor_scalar(ve2[:, :], mv2[:, :, 1], EPS, None, ALU.add).then_inc(var2, 1)

            def x1_final(g, b, cs):
                s = NB * g + b
                if cs[0] == 0:
                    dve.wait_ge(rstd2, s + 1)
                    dve.wait_ge(res_done, s + 1)
                for c in cs:
                    nc.vector.scalar_tensor_tensor(out=xres[b][:, c, 0:C], in0=cen[:, c, :],
                                                   scalar=rs2[:, c:c + 1], in1=xres[b][:, c, 0:C],
                                                   op0=ALU.mult, op1=ALU.add).then_inc(x1_made, 1)

            def x1_stats(g, b):
                dve.wait_ge(x1_made, CH * (NB * g + b) + CH)
                for c in range(CH):
                    last = nc.vector.bn_stats(st3[:, c, :], xres[b][:, c, 0:C])
                last.then_inc(stat3, 1)

            def x1_var(g, b):
                s = NB * g + b
                dve.wait_ge(stat3, s + 1)
                alone(dve, gate_dve)
                for c in range(CH):
                    last = nc.vector.bn_aggr(mv3[:, c, :], st3[:, c, :])
                last.then_inc(aggr3, 1)
                dve.wait_ge(aggr3, s + 1)
                nc.vector.tensor_scalar(nm3[:, :], mv3[:, :, 0], -1.0, None, ALU.mult)
                nc.vector.tensor_scalar(ve3[:, :], mv3[:, :, 1], EPS, None, ALU.add).then_inc(var3, 1)

            def body(g, b, front, lead, fillers=None):
                s = NB * g + b
                for c in range(1, CH - 1):
                    if fillers:
                        fillers(c - 1)
                    state_rest(b, s, c)
                    out_centred(s, c)
                    if lead and c == 1:
                        for i in range(CH):
                            lead_stat(g + 1, b, i)
                        lead_var(g + 1, b)
                    if lead and c == 2:
                        lead_norm(g + 1, b, False)
                    if front:
                        h_rest(s + 1, 2 * c - 2)
                if fillers:
                    fillers(CH - 2)
                out_centred(s, CH - 1)
                out_var(s)
                if front:
                    h_rest(s + 1, 4)
                    q_rest(1 - b, s + 1)
                state_rest(b, s, CH - 1)
                x1_final(g, b, (0, 1))
                if front:
                    k_rest(s + 1)
                    v_biased(s + 1, 0)
                    v_biased(s + 1, 1)
                    ktok_rest(1 - b, s + 1)
                    scores_masked(s + 1)
                x1_final(g, b, (2,))
                if front:
                    scores_rest(s + 1)
                if lead:
                    xnT_rest(s + 2)
                if front:
                    state_rest(1 - b, s + 1, 0)
                    out_centred(s + 1, 0)
                x1_final(g, b, (3,))
                x1_stats(g, b)
                x1_var(g, b)

            for b in range(NB):
                nc.vector.memset(s_ps[b][:, :], 0.0).then_inc(zeroed, 1)
            for b in range(NB):
                last = nc.vector.memset(state[b][:, :, :].bitcast(F32), 0.0)
            last.then_inc(s_lo, 1)
            dve.sem_inc(o_cen, 2)
            for c in range(CH):
                lead_stat(0, 0, c)
            lead_var(0, 0)
            lead_norm(0, 0, True)

            def weights_rest(ws):
                for i in ws:
                    dve.wait_ge(w_hi, i + 1)
                    nc.vector.tensor_tensor(w_sp[:, i, 1, :, :], w_stage[:, i, :, :],
                                            w_sp[:, i, 0, :, :].bitcast(F32), ALU.subtract).then_inc(w_lo, 1)

            dve.wait_ge(w_in[3], 16)
            nc.vector.tensor_scalar(w_stage[:, 3, :, :], w_stage[:, 3, :, :], INV_SCALE, None,
                                    ALU.mult).then_inc(w_scaled, 1)
            weights_rest((0, 1))
            xnT_rest(0)
            weights_rest((2, 3, 4, 5))
            dve.wait_ge(small_in, 16 * 8)
            nc.vector.tensor_scalar(b2c[:, Q, :], b2c[:, Q, :], INV_SCALE, None, ALU.mult).then_inc(w_scaled, 1)
            for c in range(CH):
                lead_stat(0, 1, c)
            lead_var(0, 1)
            for m in (0, 2, 4):
                h_rest(0, m)
            dve.wait_ge(w_scaled, 2)
            q_rest(0, 0)
            lead_norm(0, 1, False)
            k_rest(0)
            v_biased(0, 0)
            v_biased(0, 1)
            ktok_rest(0, 0)
            dve.wait_ge(consts, 4)
            scores_masked(0)
            scores_rest(0)
            xnT_rest(1)
            state_rest(0, 0, 0)
            out_centred(0, 0)
            with dve.Fori(0, STEPS // NB - 1) as g:
                for b in range(NB):
                    body(g, b, True, True)
            body(STEPS // NB - 1, 0, True, False)

            done = [0]

            def link(ins):
                done[0] += 1
                ins.then_inc(rv, 1)
                dve.wait_ge(rv, done[0])

            def tile_rest(ts):
                for t in ts:
                    dve.wait_ge(wf_hi, t + 1)
                    nc.vector.tensor_tensor(wf_sp[:, t, 1, :], ring[t % 3][:, :], wf_sp[:, t, 0, :].bitcast(F32),
                                            ALU.subtract).then_inc(wf_lo, 1)

            def over_t(a):
                return a.unsqueeze(1).broadcast_to([P, NT, NJ])

            def over_j(a):
                return a.unsqueeze(2).broadcast_to([P, NT, NJ])

            def by_j(a):
                return a.rearrange("p t j -> p j t")

            def route_signs():
                dve.wait_ge(route_in, 64)
                link(nc.vector.tensor_scalar(sgn[:, 0, :], sig_in[:, :], 0.0, None, ALU.is_gt))
                link(nc.vector.tensor_scalar(sgn[:, 1, :], sig_in[:, :], 0.0, None, ALU.is_lt))
                link(nc.vector.tensor_tensor(sgn[:, 2, :], sgn[:, 0, :], sgn[:, 1, :], ALU.subtract))

            def route_argmax():
                dve.wait_ge(rp, 1)
                dve.wait_ge(rconst, 7)
                link(nc.vector.tensor_copy(rsc[:, :, :], sc_ps[:, 0:NJ * NT].rearrange("p (j t) -> p t j", t=NT)))
                link(nc.vector.tensor_reduce(rmax[:, :], by_j(rsc[:, :, :]), AX_X, ALU.max))
                link(nc.vector.tensor_tensor(req[:, :, :], rsc[:, :, :], over_t(rmax[:, :]), ALU.is_ge))
                link(nc.vector.tensor_tensor(rcand[:, :, :], req[:, :, :], revt[:, :, :], ALU.mult))
                link(nc.vector.tensor_reduce(rbest[:, :], by_j(rcand[:, :, :]), AX_X, ALU.max))
                link(nc.vector.tensor_tensor(onehot[:, :, :], revt[:, :, :], over_t(rbest[:, :]), ALU.is_equal))

            def route_slots():
                dve.wait_ge(rp, 2)
                link(nc.vector.tensor_copy(tot[:, :, :], sc_ps[:, 256:384].rearrange("p (t j) -> p t j", t=NT)))
                link(nc.vector.tensor_tensor_scan(incl[:, :, :].rearrange("p t j -> p (t j)"),
                                                  keep[:, :, :].rearrange("p t j -> p (t j)"),
                                                  tot[:, :, :].rearrange("p t j -> p (t j)"), 0.0,
                                                  ALU.mult, ALU.add))
                link(nc.vector.tensor_tensor(blk_gt[:, :, :], over_j(incl[:, :, NJ - 1]), blk_edge[:, :, :],
                                             ALU.is_gt))
                link(nc.vector.tensor_reduce(blks[:, :], blk_gt[:, :, :], AX_X, ALU.add))
                link(nc.vector.tensor_tensor_scan(ends[:, :], keep8[:, :], blks[:, :], 0.0, ALU.mult, ALU.add))
                link(nc.vector.tensor_tensor(starts[:, :], ends[:, :], blks[:, :], ALU.subtract))
                link(nc.vector.tensor_scalar(starts[:, :], starts[:, :], float(P), None, ALU.mult))
                link(nc.vector.tensor_tensor(zed[:, :, :], incl[:, :, :], tot[:, :, :], ALU.subtract))
                link(nc.vector.tensor_tensor(zed[:, :, :], zed[:, :, :], over_j(starts[:, :]), ALU.add))
                link(nc.vector.tensor_tensor(zed[:, :, :], sc_ps[:, 128:256].rearrange("p (t j) -> p t j", t=NT),
                                             zed[:, :, :], ALU.add))
                link(nc.vector.tensor_tensor(slot_t[:, :, :], zed[:, :, :], onehot[:, :, :], ALU.mult))
                link(nc.vector.tensor_reduce(slot[:, :], by_j(slot_t[:, :, :]), AX_X, ALU.add))
                dve.wait_ge(rconst, 9)
                link(nc.vector.tensor_tensor(above[:, :, :], slot[:, :].unsqueeze(2).broadcast_to([P, NJ, NBLK + 1]),
                                             edges[:, :, :], ALU.is_ge))
                link(nc.vector.tensor_tensor(inblk[:, :, :], above[:, :, 0:NBLK], above[:, :, 1:NBLK + 1],
                                             ALU.subtract))
                link(nc.vector.tensor_tensor(poscol[:, :, :], inblk[:, :, :],
                                             posn[:, :].unsqueeze(2).broadcast_to([P, NJ, NBLK]), ALU.mult))
                link(nc.vector.tensor_reduce(nblk[:, :], above[:, :, 1:NBLK], AX_X, ALU.add))
                link(nc.vector.scalar_tensor_tensor(out=rest[:, :], in0=nblk[:, :], scalar=-float(P), in1=slot[:, :],
                                                    op0=ALU.mult, op1=ALU.add))
                for j in range(NJ):
                    done[0] += 1
                    nc.vector.tensor_scalar(lane_oh[j], lane[:, :], rest[:, j:j + 1], None,
                                            ALU.is_equal).then_inc(rv, 1)

            def route_tables():
                link(nc.vector.tensor_tensor(kge[:, :, :], kcol[:, :, :],
                                             ends[0:1, :].unsqueeze(1).broadcast_to([1, NBLK, NT]), ALU.is_ge))
                link(nc.vector.tensor_reduce(tile_f[:, 0, :], kge[:, :, :], AX_X, ALU.add))
                link(nc.vector.tensor_scalar(tile_f[:, 1, :], tile_f[:, 0, :], float(NT - 1), None, ALU.min))
                link(nc.vector.tensor_copy(tile_i[:, :], tile_f[:, 1, :]))
                dve.wait_ge(rp, 3)
                link(nc.vector.tensor_copy(idx_f[:, 0, :], sc_ps[:, 0:NBLK]))
                link(nc.vector.tensor_scalar(idx_f[:, 1, :], idx_f[:, 0, :], -1.0, 0.0, ALU.add, ALU.max))
                link(nc.vector.tensor_scalar(idx_f[:, 2, :], idx_f[:, 0, :], 0.0, float(FAR), ALU.is_equal, ALU.mult))
                link(nc.vector.scalar_tensor_tensor(out=idx_f[:, 3, :], in0=idx_f[:, 0, :], scalar=-1.0,
                                                    in1=idx_f[:, 2, :], op0=ALU.add, op1=ALU.add))
                link(nc.vector.tensor_scalar(idx_f[:, 4, :], idx_f[:, 3, :], float(T), None, ALU.add))
                link(nc.vector.tensor_copy(idx_i[:, 0:NBLK], idx_f[:, 1, :]))
                link(nc.vector.tensor_copy(idx_i[:, NBLK:3 * NBLK].rearrange("p (b k) -> p b k", b=NB), idx_f[:, 3:5, :]))

            def fillers(n):
                if n == 0:
                    route_argmax()
                    tile_rest((0, 1))
                if n == 1:
                    route_slots()
                    tile_rest((2, 3))
                if n == 2:
                    route_tables()

            route_signs()
            body(STEPS // NB - 1, 1, False, False, fillers)
            tile_rest(range(4, NT))

            def block_residual(turn, p, first):
                n = RB * turn + p
                t = dve.value_load(tile_i[0:1, bass.ds(n, 1)], min_val=0, max_val=NT - 1)
                dve.wait_ge(got[p], 16 * turn + 16)
                if not first:
                    dve.wait_ge(y_done, n - RB + 1)
                nc.vector.tensor_tensor(resb[p], grow[p].rearrange("p (b d) -> p b d", b=NB)[:, :, 0:C],
                                        bias_rows[:, bass.ds(t, 1), :].broadcast_to([P, NB, C]), ALU.add)
                nc.vector.tensor_copy(gidx[p][:, :], idx_i[:, bass.ds(n + RB, 1)]).then_inc(resb_done, 1)

            def block_rest(n, p):
                dve.wait_ge(xb_hi, n + 1)
                nc.vector.tensor_tensor(xbT[p][:, 1, :], t_bank[p][:, :], xbT[p][:, 0, :].bitcast(F32),
                                        ALU.subtract).then_inc(xb_lo, 1)

            def block_out(turn, p, first):
                n = RB * turn + p
                dve.wait_ge(y_ps, n + 1)
                dve.wait_ge(resb_done, n + 1)
                if not first:
                    dve.wait_ge(sent[p], 32 * turn)
                nc.vector.tensor_copy(sidx[p][:, :], idx_i[:, NBLK:3 * NBLK].rearrange("p (b k) -> p b k", b=NB)
                                      [:, :, bass.ds(n, 1)].rearrange("p b k -> p (b k)"))
                nc.vector.tensor_tensor(yb[p].rearrange("p b d -> p (b d)"), y_bank[p][:, :],
                                        resb[p].rearrange("p b d -> p (b d)"), ALU.add).then_inc(y_done, 1)

            block_residual(0, 0, True)

            def one_slot(turn, j, edge):
                n = RB * turn + j
                if not edge or n < NBLK:
                    block_rest(n, j)
                if not edge or n > 0:
                    block_out(turn + (j - 1) // RB, (j - 1) % RB, edge and n - 1 < RB)
                if not edge or n + 1 < NBLK:
                    block_residual(turn + (j + 1) // RB, (j + 1) % RB, edge and n + 1 < RB)

            over_slots(dve, one_slot)

        @block.gpsimd
        def _(pool):
            nc.gpsimd.memset(ident[:, :], 0.0).then_inc(consts, 1)
            pool.wait_ge(consts, 1)
            nc.gpsimd.affine_select(out=ident[:, :], in_=ident[:, :], compare_op=ALU.not_equal, fill=1.0, base=0,
                                    pattern=[[-1, P]], channel_multiplier=1).then_inc(consts, 1)
            nc.gpsimd.memset(half[:, :], -0.5).then_inc(consts, 1)
            nc.gpsimd.memset(tril[:, :], 1.0).then_inc(rconst, 1)
            pool.wait_ge(rconst, 1)

            def rstd_lead(s):
                pool.wait_ge(var1, s + 1)
                nc.gpsimd.tensor_tensor(rs1[:, :], ve1[:, :], half[:, :], ALU.pow).then_inc(rstd1, 1)

            def residual(g, b, first):
                pool.wait_ge(x_in[b], 16 * (g + 1))
                if not first:
                    pool.wait_ge(x1_out[b], 16 * (g + b))
                nc.gpsimd.tensor_tensor(xres[b][:, :, 0:C], xt[b][:, :, :],
                                        lnb_row[:, :].unsqueeze(1).broadcast_to([P, CH, C]),
                                        ALU.add).then_inc(res_done, 1)

            def h_rest(s, m):
                pool.wait_ge(h_hi, 6 * s + m + 1)
                nc.gpsimd.tensor_tensor(hT[:, m, 1, :], h32[:, m, :], hT[:, m, 0, :].bitcast(F32),
                                        ALU.subtract).then_inc(h_lo_pool, 1)

            def v_rest(b, s):
                for j in range(2):
                    pool.wait_ge(v_hi, 2 * s + 1 + j)
                    nc.gpsimd.tensor_tensor(vtok[b][:, 1, 2 * j:2 * j + 2, :], v32[:, 2 * j:2 * j + 2, :],
                                            vtok[b][:, 0, 2 * j:2 * j + 2, :].bitcast(F32),
                                            ALU.subtract).then_inc(v_lo, 1)

            def rstd_out(s):
                pool.wait_ge(var2, s + 1)
                nc.gpsimd.tensor_tensor(rs2[:, :], ve2[:, :], half[:, :], ALU.pow).then_inc(rstd2, 1)

            def rstd_x1(b, s):
                pool.wait_ge(var3, s + 1)
                nc.gpsimd.tensor_tensor(xres[b][:, :, C + 1], ve3[:, :], half[:, :], ALU.pow).then_inc(rstd3, 1)
                pool.wait_ge(rstd3, s + 1)
                nc.gpsimd.tensor_tensor(xres[b][:, :, C], nm3[:, :], xres[b][:, :, C + 1], ALU.mult
                                        ).then_inc(shift3, 1)

            def body(g, b, front, lead):
                s = NB * g + b
                if lead:
                    rstd_lead(s + 2)
                if front:
                    h_rest(s + 1, 1)
                    residual(g + b, 1 - b, False)
                    h_rest(s + 1, 3)
                    h_rest(s + 1, 5)
                rstd_out(s)
                if front:
                    v_rest(1 - b, s + 1)
                rstd_x1(b, s)

            pool.wait_ge(consts, 3)
            rstd_lead(0)
            nc.gpsimd.affine_select(out=tril[:, :], in_=tril[:, :], compare_op=ALU.is_ge, fill=0.0, base=0,
                                    pattern=[[1, P]], channel_multiplier=-1).then_inc(consts, 1)
            pool.wait_ge(small_in, 16 * 8)
            residual(0, 0, True)
            rstd_lead(1)
            pool.sem_inc(x1_out[1], 16)
            for m in (1, 3, 5):
                h_rest(0, m)
            v_rest(0, 0)
            with pool.Fori(0, STEPS // NB - 1) as g:
                for b in range(NB):
                    body(g, b, True, True)

            nc.gpsimd.memset(ones[:, :], 1.0).then_inc(rconst, 1)
            nc.gpsimd.memset(keep8[:, :], 1.0)
            nc.gpsimd.memset(keep[:, :, :], 1.0).then_inc(rconst, 1)
            pool.wait_ge(rconst, 3)
            nc.gpsimd.memset(keep[:, :, 0:1], 0.0).then_inc(rconst, 1)
            nc.gpsimd.affine_select(out=lower[:, :], in_=ones[:, :], compare_op=ALU.is_gt, fill=0.0, base=0,
                                    pattern=[[1, P]], channel_multiplier=-1).then_inc(rconst, 1)
            exact = dict(allow_small_or_imprecise_dtypes=True)
            nc.gpsimd.iota(revt[:, :, :], [[-1, NT], [0, NJ]], base=NT, channel_multiplier=0, **exact)
            nc.gpsimd.iota(blk_edge[:, :, :], [[0, NT], [P, NJ]], base=0, channel_multiplier=0, **exact
                           ).then_inc(rconst, 1)
            nc.gpsimd.iota(lane[:, :], [[1, P]], base=0, channel_multiplier=0, **exact)
            nc.gpsimd.iota(posn[:, :], [[P, NJ]], base=1, channel_multiplier=1, **exact).then_inc(rconst, 1)

            body(STEPS // NB - 1, 0, True, False)
            pool.wait_ge(k_lo, 2 * STEPS)
            pool.wait_ge(fill, FILLS * STEPS)
            nc.gpsimd.iota(edges[:, :, :], [[0, NJ], [P, NBLK + 1]], base=0, channel_multiplier=0, **exact
                           ).then_inc(rconst, 1)
            nc.gpsimd.iota(kcol[:, :, :], [[1, NBLK], [0, NT]], base=0, channel_multiplier=0, **exact
                           ).then_inc(rconst, 1)
            body(STEPS // NB - 1, 1, False, False)

            def gather(n, p, first):
                if not first:
                    pool.wait_ge(xnb_done, n - RB + 1)
                    pool.wait_ge(resb_done, n - RB + 1)
                    alone(pool, gate_pool)
                pool.indirect_dma_start(out=grow[p], out_offset=None, in_=scratch,
                                        in_offset=bass.IndirectOffsetOnAxis(
                                            ap=idx_i[:, n:n + 1] if first else gidx[p][:, :], axis=0)
                                        ).then_inc(got[p], 16)

            def scatter(n, p):
                pool.wait_ge(y_done, n + 1)
                alone(pool, gate_pool)
                for b in range(NB):
                    pool.indirect_dma_start(out=out_rows, out_offset=bass.IndirectOffsetOnAxis(
                                                ap=sidx[p][:, b:b + 1], axis=0),
                                            in_=yb[p][:, b, :], in_offset=None, bounds_check=NB * T - 1,
                                            oob_is_err=False).then_inc(sent[p], 16)

            pool.wait_ge(rv, ROUTED)
            for b in range(NB):
                pool.wait_ge(x1_out[b], 16 * (STEPS // NB + b))
            for n in range(RB):
                gather(n, n, True)

            def one_slot(turn, j, edge):
                n = RB * turn + j
                if not edge or n + RB < NBLK:
                    gather(n + RB, j, False)
                if not edge or n > 0:
                    scatter(n - 1, (j - 1) % RB)

            over_slots(pool, one_slot)
            for p in range(RB):
                pool.wait_ge(sent[p], 32 * ((NBLK - p + RB - 1) // RB))


def position_table(seq, dim):
    import math
    import numpy as np
    pos = np.arange(seq, dtype=np.float32)[:, None]
    step = np.arange(0, dim, 2, dtype=np.float32) * np.float32(-math.log(10000.0) / dim)
    angle = (pos * np.exp(step.astype(np.float64)).astype(np.float32)).astype(np.float64)
    table = np.zeros((seq, dim), dtype=np.float32)
    table[:, 0::2] = np.sin(angle)
    table[:, 1::2] = np.cos(angle)
    return np.ascontiguousarray(table.T)


_INS = ['L0_attn_x', 'L0_attn_W1q', 'L0_attn_b1q', 'L0_attn_W2q', 'L0_attn_b2q', 'L0_attn_W1k', 'L0_attn_b1k',
        'L0_attn_W2k', 'L0_attn_b2k', 'L0_attn_W1v', 'L0_attn_b1v', 'L0_attn_W2v', 'L0_attn_b2v', 'L0_attn_ln_w',
        'L0_attn_ln_b', 'L0_ffn_tile_sigs', 'L0_ffn_W', 'L0_ffn_b']


def kernel(**inputs):
    import numpy as _np
    import concourse.bacc as _bacc
    from concourse import mybir as _mybir
    from concourse.bass_utils import run_bass_kernel_spmd as _run

    nc = _bacc.Bacc("TRN2", target_bir_lowering=False, num_devices=1)
    arrays, ap = {}, {}
    for name in _INS:
        a = _np.ascontiguousarray(inputs[name])
        arrays[f"in_{name}_dram"] = a
        ap[name] = nc.dram_tensor(f"in_{name}_dram", a.shape, _mybir.dt.from_np(a.dtype), kind="ExternalInput").ap()
    arrays["position_table"] = position_table(T, DP)
    pe = nc.dram_tensor("position_table", (DP, T), F32, kind="ExternalInput").ap()
    out = nc.dram_tensor("out_0_dram", (NB, T, C), F32, kind="ExternalOutput").ap()
    mk_seq_kernel(nc, ap['L0_attn_x'], [ap[f'L0_attn_W1{n}'] for n in 'qkv'], [ap[f'L0_attn_b1{n}'] for n in 'qkv'],
                  [ap[f'L0_attn_W2{n}'] for n in 'qkv'], [ap[f'L0_attn_b2{n}'] for n in 'qkv'],
                  ap['L0_attn_ln_w'], ap['L0_attn_ln_b'], ap['L0_ffn_tile_sigs'], ap['L0_ffn_W'], ap['L0_ffn_b'],
                  pe, out)
    r = _run(nc, [arrays], core_ids=[0])
    return r.results[0]["out_0_dram"]
```

```python
from contextlib import ExitStack

import concourse.bass as bass
from concourse import mybir

F32 = mybir.dt.float32
F32R = mybir.dt.float32r
I32 = mybir.dt.int32
ALU = mybir.AluOpType
ACT = mybir.ActivationFunctionType
AX_X = mybir.AxisListType.X

P = 128
NB = 2
T = 2048
C = 256
KC = C // P
GT = 512
CH = GT // P
STEPS = NB * T // GT
NT = 8
DP = 32
LOW = 32
EPS = 1e-5
INV_SCALE = float((C * 512) ** -0.5)
NJ = T // P
ROW = C + 2
NPAIR = NJ + NT - 1
FILLS = 16
WARM = (24, 15, 8, 16)
SPLIT = ((0, 0), (0, 1), (1, 0))
Q, K, V = range(3)
RB = 4
ROWS_ROUTED = 33
ROUTED = 46


def mk_seq_kernel(nc, x, w1, w2, bias_cols, rows3, sigs2, ffn_w, ffn_b, pe, out):
    scratch = nc.dram_tensor("x1_rows", [T, NB * ROW], F32, kind="Internal").ap()
    rows_sbp = scratch.rearrange("(g c p) (b d) -> g b p c d", p=P, c=CH, b=NB)
    x_gbp = x.rearrange("b (g c p) d -> g b p c d", p=P, c=CH)
    out_rows = out.rearrange("b s d -> (b s) d")

    with ExitStack() as ctx:
        def sb(name, shape, dt=F32):
            return ctx.enter_context(nc.sbuf_tensor(name, shape, dt))

        def sem(name):
            return ctx.enter_context(nc.semaphore(name))

        w_stage = sb("w_stage", [P, 6, KC, C])
        w_all = sb("w_all", [P, NT, 2, KC * C], F32R)
        w_sp = w_all[:, 0:6].rearrange("p m a (k c) -> p m a k c", k=KC)
        wf_sp = w_all
        b_cols = sb("b_cols", [P, 5, KC])
        b1c = b_cols[:, 0:3]
        b2c = b_cols[:, 3:5]
        row_stage = sb("row_stage", [P, 3, C])
        lnw_row, lnb_row, b2v_row = [row_stage[:, i] for i in range(3)]
        warm = sb("warm", [P, 1])
        ident = sb("ident", [P, P])
        tril = sb("tril", [P, P])
        half = sb("half", [P, CH])
        xt = [sb(f"xt{b}", [P, CH, C]) for b in range(NB)]
        xres = [sb(f"xres{b}", [P, CH, ROW]) for b in range(NB)]
        xn = sb("xn", [P, CH, C])
        st1 = sb("st1", [P, CH, 6])
        mv1 = sb("mv1", [P, CH, 2])
        ve1 = sb("ve1", [P, CH])
        rs1 = sb("rs1", [P, CH])
        h32 = sb("h32", [P, 6, GT])
        hT = sb("hT", [P, 6, 2, GT], F32R)
        peT = hT[0:2 * DP, 0:2].rearrange("p m a n -> p (m a n)")
        k32 = sb("k32", [P, KC, GT])
        v32 = sb("v32", [P, CH, C])
        sc32 = sb("sc32", [P, GT])
        cen = sb("cen", [P, CH, C])
        st2 = sb("st2", [P, CH, 6])
        mv2 = sb("mv2", [P, CH, 2])
        ve2 = sb("ve2", [P, CH])
        rs2 = sb("rs2", [P, CH])
        st3 = sb("st3", [P, CH, 6])
        mv3 = sb("mv3", [P, CH, 2])
        ve3 = sb("ve3", [P, CH])
        nm3 = sb("nm3", [P, CH])

        ring = [ctx.enter_context(nc.psum_tensor(f"ring{i}", [P, 512], F32)) for i in range(3)]
        sc_ps = ctx.enter_context(nc.psum_tensor("sc_ps", [P, 512], F32))
        o_ps = [ctx.enter_context(nc.psum_tensor(f"o_ps{i}", [P, 512], F32)) for i in range(2)]
        s_ps = [ctx.enter_context(nc.psum_tensor(f"s_ps{b}", [P, 512], F32)) for b in range(NB)]

        x_in = [sem(f"x_in{b}") for b in range(NB)]
        w_in = [sem(f"w_in{i}") for i in range(6)]
        small_in = sem("small_in")
        ffn_in = [sem(f"ffn_in{i}") for i in range(3)]
        sigs_in = sem("sigs_in")
        table_in = sem("table_in")
        bias_in = sem("bias_in")
        consts = sem("consts")
        zeroed = sem("zeroed")
        w_scaled = sem("w_scaled")
        w_hi = sem("w_hi")
        w_lo = sem("w_lo")
        stat1 = sem("stat1")
        aggr1 = sem("aggr1")
        var1 = sem("var1")
        rstd1 = sem("rstd1")
        xn_done = sem("xn_done")
        res_done = sem("res_done")
        fill = sem("fill")
        xnT_hi = sem("xnT_hi")
        xnT_lo = sem("xnT_lo")
        gelu = sem("gelu")
        h_hi = sem("h_hi")
        h_lo_dve = sem("h_lo_dve")
        h_lo_pool = sem("h_lo_pool")
        q_hi = sem("q_hi")
        q_lo = sem("q_lo")
        k_full = sem("k_full")
        k_hi = sem("k_hi")
        k_lo = sem("k_lo")
        v_sum = sem("v_sum")
        v_hi = sem("v_hi")
        v_lo = sem("v_lo")
        ktok_hi = sem("ktok_hi")
        ktok_lo = sem("ktok_lo")
        scores = sem("scores")
        sc_mask = sem("sc_mask")
        sc_hi = sem("sc_hi")
        sc_lo = sem("sc_lo")
        o_ready = sem("o_ready")
        s_ready = sem("s_ready")
        s_hi = sem("s_hi")
        s_lo = sem("s_lo")
        o_stat = sem("o_stat")
        o_aggr = sem("o_aggr")
        o_cen = sem("o_cen")
        var2 = sem("var2")
        rstd2 = sem("rstd2")
        x1_made = sem("x1_made")
        stat3 = sem("stat3")
        aggr3 = sem("aggr3")
        var3 = sem("var3")
        rstd3 = sem("rstd3")
        shift3 = sem("shift3")
        x1_out = [sem(f"x1_out{b}") for b in range(NB)]

        sgn = sb("sgn", [2 * DP, 2, NT])
        sgn_r = sb("sgn_r", [2 * DP, NT], F32R)
        sig_in = sb("sig_in", [2 * DP, NT])
        bias_raw = [k32[0:LOW + 1, :, :].rearrange("p k n -> p (k n)"), h32[0:LOW + 1, 4:6, :].rearrange("p m n -> p (m n)")]
        bias_hl = sb("bias_hl", [LOW + 1, 2, NT * C // 2], F32R)
        ones_r = sb("ones_r", [LOW + 1, P], F32R)
        h_flat = h32[:, :, :].rearrange("p m n -> p (m n)")
        w_flat = w_stage[:, :, :, :].rearrange("p a k c -> p (a k c)")
        carved = [0]

        def carve(*dims, parts=P):
            n, at = 1, carved[0]
            for d in dims:
                n *= d
            carved[0] += n
            names = "abc"[:len(dims)]
            return w_flat[0:parts, at:at + n].rearrange(f"p ({' '.join(names)}) -> p {' '.join(names)}",
                                                        **dict(zip(names, dims)))

        rsc = carve(NT, NJ)
        rmax = sb("rmax", [P, NJ])
        req = carve(NT, NJ)
        rcand = carve(NT, NJ)
        rbest = sb("rbest", [P, NJ])
        onehot = carve(NT, NJ)
        lower = sb("lower", [P, P])
        ones = sb("ones", [P, P])
        revt = sb("revt", [P, NT, NJ])
        keep = sb("keep", [P, NT, NJ])
        ranks = carve(2, NT, NJ)
        incl = carve(NT, NJ)
        zed = carve(NT, NJ)
        slot_t = carve(NT, NJ)
        slot = sb("slot", [P, NJ])
        blk_edge = sb("blk_edge", [P, NT, NJ])
        blk_gt = carve(NT, NJ)
        keep8 = sb("keep8", [P, NT])
        sums8 = sb("sums8", [P, 5, NT])
        blk_end, blk_first, pairs8, upto8, before8 = [sums8[:, i] for i in range(5)]
        tile_q = sb("tile_q", [P, 4, NT])
        starts, ends, base8, number8 = [tile_q[:, i] for i in range(4)]
        pcol = carve(NPAIR, NT)
        pge = carve(2, NPAIR, NT)
        pair_t = carve(NPAIR, NT)
        pair_q = carve(4, NPAIR)
        pair_f = carve(5, NPAIR)
        mask = sb("mask", [P, NPAIR])
        pair_i = sb("pair_i", [1, 2, NPAIR], I32)
        edges = carve(NJ, NJ + 1)
        above = carve(NJ, NJ + 1)
        inblk = w_flat[:, 0:NJ * NJ].rearrange("p (j k) -> p j k", j=NJ)
        pair_m = w_flat[:, 0:4 * NPAIR * NT].rearrange("p (q n t) -> p q n t", q=4, n=NPAIR)
        posn = sb("posn", [P, NJ])
        poscol = carve(NJ, NJ)
        nblk = sb("nblk", [P, NJ])
        rest = sb("rest", [P, NJ])
        lane = sb("lane", [P, P])
        lane_p = sb("lane_p", [P, 1])
        lane_oh = [(xn if j < CH * KC else v32)[:, j // KC % CH, j % KC * P:j % KC * P + P] for j in range(NJ)]
        idx_i = sb("idx_i", [P, NB, NJ], I32)
        x_stage = [xt[i][:, :, :].rearrange("p (t k) c -> p t k c", t=2) for i in range(2)]
        h_stage = h_flat[:, 0:4 * KC * C].rearrange("p (t k c) -> p t k c", t=4, k=KC)
        ffn_stage = [x_stage[t // 2][:, t % 2] if t < 4 else h_stage[:, t - 4] for t in range(NT)]
        xnb = [a[:, i:i + NB] for a in (xn, v32) for i in (0, NB)]
        xbT = [hT[:, i] for i in range(RB)]
        t_bank = ring + [s_ps[0]]
        y_bank = o_ps + [sc_ps, s_ps[1]]

        attention = ExitStack()

        def sb_a(name, shape, dt):
            return attention.enter_context(nc.sbuf_tensor(name, shape, dt))

        xnT = sb_a("xnT", [P, 2, KC, GT], F32R)
        qT = [sb_a(f"qT{b}", [P, 2, KC, GT], F32R) for b in range(NB)]
        kT = sb_a("kT", [P, 2, KC, GT], F32R)
        ktok = [sb_a(f"ktok{b}", [P, 2, CH, C], F32R) for b in range(NB)]
        vtok = [sb_a(f"vtok{b}", [P, 2, CH, C], F32R) for b in range(NB)]
        scT = sb_a("scT", [P, 2, GT], F32R)
        state = [sb_a(f"state{b}", [P, 2, KC * C], F32R) for b in range(NB)]
        attention.close()
        rows = sb("block_rows", [P, NJ, NB * ROW])
        acc = sb("acc", [P, NJ, NB * C])

        rconst = sem("rconst")
        rv = sem("rv")
        lanes = sem("lanes")
        rp = sem("rp")
        wf_t = sem("wf_t")
        wf_hi = sem("wf_hi")
        wf_lo = sem("wf_lo")
        got = [sem(f"got{i}") for i in range(RB)]
        sent = sem("sent")
        rows_in = sem("rows_in")
        xnb_done = sem("xnb_done")
        copy_in = [sem(f"copy_in{i}") for i in range(2)]
        copied = sem("copied")
        bias_hi = sem("bias_hi")
        bias_lo = sem("bias_lo")
        ones_set = sem("ones_set")
        xb_t = sem("xb_t")
        xb_hi = sem("xb_hi")
        xb_lo = sem("xb_lo")
        y_ps = sem("y_ps")
        y_done = sem("y_done")

        gate_dve = sem("gate_dve")

        block = ctx.enter_context(nc.Block())

        def alone(eng, gate):
            eng.sem_inc(gate, 1)

        def cols(c):
            return slice(c * P, (c + 1) * P)

        def over_slots(eng, one_slot):
            head = RB + 1
            loops = (NPAIR - 1 - head) // RB
            for k in range(head):
                one_slot(k // RB, k % RB, True)
            with eng.Fori(0, loops) as i:
                for k in range(head, head + RB):
                    one_slot(i + k // RB, k % RB, False)
            for k in range(head + RB * loops, NPAIR + 1):
                one_slot(k // RB, k % RB, True)

        @block.sync
        def _(sp):
            def load_x(g, b):
                sp.dma_start(xt[b][:, :, :], x_gbp[bass.ds(g, 1), b].rearrange("g p c d -> p (g c) d")
                             ).then_inc(x_in[b], 16)

            def store(g, b):
                sp.wait_ge(shift3, NB * g + b + 1)
                sp.dma_start(rows_sbp[bass.ds(g, 1), b].rearrange("g p c d -> p (g c) d"), xres[b][:, :, :]
                             ).then_inc(x1_out[b], 16)

            load_x(0, 0)
            for i, w in enumerate((w1[Q], w1[K], w1[V], w2[Q], w2[K], w2[V])):
                sp.dma_start(w_stage[:, i, :, :], w.rearrange("(k p) n -> p k n", p=P)).then_inc(w_in[i], 16)
                if i == 2:
                    load_x(0, 1)
            sp.wait_ge(xn_done, 1)
            sp.wait_ge(res_done, 1)
            load_x(1, 0)

            def body(g, b, front, lead):
                if lead:
                    sp.wait_ge(xn_done, NB * g + b + 2)
                    sp.wait_ge(res_done, NB * g + b + 2)
                    load_x(g + 1 + b, 1 - b)
                store(g, b)

            with sp.Fori(0, STEPS // NB - 2) as g:
                for b in range(NB):
                    body(g, b, True, True)
            body(STEPS // NB - 2, 0, True, True)
            body(STEPS // NB - 2, 1, True, False)
            ffn_v = ffn_w.rearrange("t (k p) d -> p t k d", p=P)
            sp.wait_ge(xn_done, STEPS)
            sp.wait_ge(res_done, STEPS)
            for i in range(2):
                sp.dma_start(x_stage[i], ffn_v[:, 2 * i:2 * i + 2]).then_inc(ffn_in[i], 16)
            sp.wait_ge(h_lo_dve, 3 * STEPS)
            sp.wait_ge(h_lo_pool, 3 * STEPS)
            sp.dma_start(h_stage, ffn_v[:, 4:8]).then_inc(ffn_in[2], 16)
            sp.wait_ge(k_lo, 2 * STEPS)
            sp.wait_ge(fill, FILLS * STEPS)
            for i in range(2):
                sp.dma_start(bias_raw[i], ffn_b.rearrange("(i t) d -> i (t d)", i=2)[i].partition_broadcast(LOW + 1)
                             ).then_inc(bias_in, 16)
            body(STEPS // NB - 1, 0, True, False)
            for part, cs in enumerate((slice(0, CH - 1), slice(CH - 1, CH))):
                sp.wait_ge(shift3, STEPS + part)
                sp.dma_start(rows_sbp[STEPS // NB - 1, NB - 1, :, cs, :], xres[NB - 1][:, cs, :]
                             ).then_inc(x1_out[NB - 1], 16)

            def copy_block(n, p):
                sp.wait_ge(rows_in, n + 1)
                sp.dma_start(acc[:, bass.ds(n, 1), :].rearrange("p k (b d) -> p (k b) d", b=NB),
                             rows[:, bass.ds(n, 1), :].rearrange("p k (b d) -> p (k b) d", b=NB)[:, :, 0:C]
                             ).then_inc(copy_in[p], 16)

            def block_there(turn, p):
                sp.wait_ge(copy_in[p], 16 * turn + 16)
                sp.sem_inc(copied, 1)

            copy_block(0, 0)
            with sp.Fori(0, NJ // 2 - 1) as i:
                copy_block(2 * i + 1, 1)
                block_there(i, 0)
                copy_block(2 * i + 2, 0)
                block_there(i, 1)
            copy_block(NJ - 1, 1)
            block_there(NJ // 2 - 1, 0)
            block_there(NJ // 2 - 1, 1)
            sp.sem_inc(copied, NPAIR - NJ)

        @block.tensor
        def _(te):
            def mm3(o, lhs, rhs, start=True, stop=True, check=False):
                n = len(lhs)
                for k in range(n):
                    for i, (a, c) in enumerate(SPLIT):
                        last = te.matmul(o, lhs[k][a], rhs[k][c], start=start and k == 0 and i == 0,
                                         stop=stop and k == n - 1 and i == 2, skip_group_check=check)
                return last

            def wpair(m, k, n0, n1):
                return [w_sp[:, m, a, k, n0:n1] for a in range(2)]

            def front_transposes(s, first):
                te.wait_ge(xn_done, s + 1)
                for k in range(KC):
                    if not first:
                        te.wait_ge(v_sum if k else ktok_lo, 2 * s)
                    for c in range(CH):
                        last = te.transpose(ring[k][:, cols(c)], xn[:, c, cols(k)], ident[:, :])
                    last.then_inc(fill, 1)

            def front_h(s, ms, first):
                for m in ms:
                    if m >= 3:
                        te.wait_ge(gelu, 6 * s + m - 2)
                    if first and m % 2 == 0:
                        te.wait_ge(w_lo, m // 2 + 1)
                    for k in range(KC):
                        if m == 0:
                            te.wait_ge(xnT_lo, 2 * s + 1 + k)
                        last = mm3(ring[(2 + m) % 3][:, :], [wpair(m // 2, k, m % 2 * P, m % 2 * P + P)],
                                   [[xnT[:, a, k, :] for a in range(2)]], start=k == 0, stop=k == KC - 1)
                    last.then_inc(fill, 1)

            def front_qk(s, which, first):
                te.wait_ge(h_lo_dve, 3 * s + which + 1)
                te.wait_ge(h_lo_pool, 3 * s + which + 1)
                if first:
                    te.wait_ge(w_lo, 4 + which)
                for j in (2 * which, 2 * which + 1):
                    if j < 3:
                        te.wait_ge(gelu, 6 * s + 4 + j)
                    else:
                        te.wait_ge(q_lo, 2 * s + 1)
                    mm3(ring[(8 + j) % 3][:, :], [wpair(3 + which, k, j % 2 * P, j % 2 * P + P) for k in range(KC)],
                        [[hT[:, 2 * which + k, a, :] for a in range(2)] for k in range(KC)]).then_inc(fill, 1)

            def front_v(s, first):
                te.wait_ge(h_lo_dve, 3 * s + 3)
                te.wait_ge(h_lo_pool, 3 * s + 3)
                if first:
                    te.wait_ge(w_lo, 6)
                for j in range(2):
                    if j == 0:
                        te.wait_ge(q_lo, 2 * s + 2)
                    else:
                        te.wait_ge(k_full, 2 * s + 1)
                    for c in (2 * j, 2 * j + 1):
                        last = mm3(ring[j][:, c % 2 * C:c % 2 * C + C],
                                   [[hT[:, 4 + k, a, cols(c)] for a in range(2)] for k in range(KC)],
                                   [wpair(5, k, 0, C) for k in range(KC)])
                    last.then_inc(fill, 1)

            def front_scores(b, s, first):
                te.wait_ge(q_lo, 2 * s + 2)
                te.wait_ge(k_lo, 2 * s + 2)
                if not first:
                    te.wait_ge(sc_mask, s)
                for c in range(CH):
                    last = mm3(sc_ps[:, cols(c)], [[kT[:, a, k, cols(c)] for a in range(2)] for k in range(KC)],
                               [[qT[b][:, a, k, cols(c)] for a in range(2)] for k in range(KC)])
                last.then_inc(scores, 1)

            def front_ktok(s):
                for n in range(2):
                    if n == 0:
                        te.wait_ge(k_full, 2 * s + 2)
                    else:
                        te.wait_ge(v_sum, 2 * s + 1)
                    for i in range(4):
                        last = te.transpose(ring[(14 + n) % 3][:, cols(i)], k32[:, i % 2, cols(2 * n + i // 2)],
                                            ident[:, :])
                    last.then_inc(fill, 1)

            def back_chunk(b, s, c):
                te.wait_ge(s_lo, 4 * s + c + 1)
                te.wait_ge(o_cen, 4 * s + c + 1)
                o = o_ps[c % 2][:, 0:C]
                mm3(o, [[qT[b][:, a, k, cols(c)] for a in range(2)] for k in range(KC)],
                    [[state[b][:, a, k * C:k * C + C] for a in range(2)] for k in range(KC)], stop=False)
                if c == 0:
                    te.wait_ge(v_lo, 2 * s + 2)
                    te.wait_ge(ktok_lo, 2 * s + 2)
                vs = [vtok[b][:, a, c, :] for a in range(2)]
                for k in range(KC):
                    last = mm3(s_ps[b][:, k * C:k * C + C], [[ktok[b][:, a, c, cols(k)] for a in range(2)]], [vs],
                               start=False, check=True)
                last.then_inc(s_ready, 1)
                if c == 0:
                    te.wait_ge(sc_lo, s + 1)
                mm3(o, [[scT[:, a, cols(c)] for a in range(2)]], [vs], start=False).then_inc(o_ready, 1)

            def body(g, b, front, lead, fillers=None):
                s = NB * g + b
                if front:
                    front_transposes(s + 1, False)
                back_chunk(b, s, 0)
                for c in range(1, CH):
                    if front:
                        front_h(s + 1, (2 * c - 2, 2 * c - 1), False)
                    elif fillers:
                        fillers(c - 1)
                    back_chunk(b, s, c)
                if front:
                    front_qk(s + 1, 0, False)
                    front_qk(s + 1, 1, False)
                    front_v(s + 1, False)
                    front_ktok(s + 1)
                    front_scores(1 - b, s + 1, False)

            def route_scores():
                te.wait_ge(rv, 3)
                te.wait_ge(table_in, 16)
                for j in range(NJ):
                    last = te.matmul(sc_ps[:, j * NT:j * NT + NT], peT[:, cols(j)], sgn_r[:, :],
                                     start=True, stop=True)
                last.then_inc(rp, 1)

            def route_counts():
                te.wait_ge(rv, 9)
                te.wait_ge(rconst, 5)
                oh = onehot[:, :, :].rearrange("p t j -> p (t j)")
                te.matmul(sc_ps[:, 128:256], lower[:, :], oh, start=True, stop=True)
                te.matmul(sc_ps[:, 256:384], ones[:, :], oh, start=True, stop=True).then_inc(rp, 1)

            def route_invert():
                te.wait_ge(rv, 23)
                te.wait_ge(sc_mask, STEPS)
                for j in range(NJ):
                    te.wait_ge(lanes, j + 1)
                    last = te.matmul(sc_ps[:, 0:NJ], lane_oh[j], poscol[:, j, :], start=(j == 0),
                                     stop=(j == NJ - 1))
                last.then_inc(rp, 1)

            te.wait_ge(consts, 2)
            for i in range(WARM[0]):
                te.transpose(ring[2][:, 0:P], ident[:, :], ident[:, :])
            route_scores()
            front_transposes(0, True)
            te.wait_ge(zeroed, 2)
            front_h(0, range(6), True)
            route_counts()
            front_qk(0, 0, True)
            front_qk(0, 1, True)
            front_v(0, True)
            front_ktok(0)
            te.wait_ge(rv, 10)
            front_scores(0, 0, True)
            with te.Fori(0, STEPS // NB - 1) as g:
                for b in range(NB):
                    body(g, b, True, True)
            body(STEPS // NB - 1, 0, True, False)

            def tile_weights(t):
                te.wait_ge(ffn_in[min(t // 2, 2)], 16)
                if t < 3:
                    te.wait_ge(ktok_lo, 2 * STEPS)
                else:
                    te.wait_ge(wf_lo, t - 2)
                for k in range(KC):
                    for o in range(KC):
                        last = te.transpose(ring[t % 3][:, k * C + o * P:k * C + o * P + P],
                                            ffn_stage[t][:, o, cols(k)], ident[:, :])
                last.then_inc(wf_t, 1)

            def fillers(n):
                if n == 0:
                    for t in range(3):
                        tile_weights(t)
                else:
                    te.wait_ge(sc_mask, STEPS)
                    for i in range(WARM[1 + n]):
                        te.transpose(sc_ps[:, 0:P], ident[:, :], ident[:, :])

            body(STEPS // NB - 1, 1, False, False, fillers)
            route_invert()
            for t in range(3, NT):
                tile_weights(t)

            def block_transposes(n, p, first, edge_bank=0):
                te.wait_ge(xnb_done, n + 1)
                if edge_bank:
                    te.wait_ge(wf_lo, edge_bank)
                if not first:
                    te.wait_ge(xb_lo, n - RB + 1)
                for b in range(NB):
                    for k in range(KC):
                        last = te.transpose(t_bank[p][:, b * C + k * P:b * C + k * P + P], xnb[p][:, b, cols(k)],
                                            ident[:, :])
                last.then_inc(xb_t, 1)

            def block_products(n, p, first):
                t = te.value_load(pair_i[0:1, 0, bass.ds(n, 1)], min_val=0, max_val=NT - 1)
                te.wait_ge(xb_lo, n + 1)
                if not first:
                    te.wait_ge(y_done, n - RB + 1)
                for b in range(NB):
                    te.matmul(y_bank[p][:, b * C:b * C + C], ones_r[:, :],
                              bias_hl[:, :, :].rearrange("p i n -> p (i n)")[:, bass.ds(t * C, C)], start=True, stop=False)
                    last = mm3(y_bank[p][:, b * C:b * C + C],
                               [[xbT[p][:, a, b * C + k * P:b * C + k * P + P] for a in range(2)] for k in range(KC)],
                               [[wf_sp[:, bass.ds(t, 1), a, k * C:k * C + C].rearrange("p t c -> p (t c)")
                                 for a in range(2)] for k in range(KC)], start=False)
                last.then_inc(y_ps, 1)

            te.wait_ge(o_cen, 4 * STEPS + 2)
            for i in range(WARM[1]):
                te.transpose(o_ps[0][:, 0:P], ident[:, :], ident[:, :])
            te.wait_ge(s_lo, 4 * STEPS)
            te.wait_ge(rv, ROUTED)
            te.wait_ge(ones_set, 3)

            def one_slot(turn, j, edge):
                n = RB * turn + j
                if not edge or n < NPAIR:
                    block_transposes(n, j, edge and n < RB, NT if edge and n < RB else 0)
                if edge and n == 1:
                    te.wait_ge(wf_lo, NT)
                    te.wait_ge(bias_lo, 2)
                if not edge or n > 0:
                    block_products(n - 1, (j - 1) % RB, edge and n - 1 < RB)

            over_slots(te, one_slot)

        @block.scalar
        def _(act):
            act.dma_start(sig_in[:, :], sigs2).then_inc(sigs_in, 16)
            act.dma_start(b_cols[:, :, :].rearrange("p a k -> p (a k)"), bias_cols).then_inc(small_in, 16)
            act.dma_start(row_stage[:, :, :], rows3.partition_broadcast(P)).then_inc(small_in, 16)
            act.wait_ge(consts, 3)
            nc.scalar.activation(warm[:, :], half[:, 0:1], ACT.Gelu)

            def xnT_rounded(s):
                for k in range(KC):
                    act.wait_ge(fill, FILLS * s + 1 + k)
                    nc.scalar.copy(xnT[:, 0, k, :], ring[k][:, :]).then_inc(xnT_hi, 1)

            def gelus(s, ms):
                for m in ms:
                    act.wait_ge(fill, FILLS * s + 3 + m)
                    nc.scalar.activation(h32[:, m, :], ring[(2 + m) % 3][:, :], ACT.Gelu,
                                         bias=b1c[:, m // 2, m % 2:m % 2 + 1]).then_inc(gelu, 1)

            def h_rounded(s, m):
                act.wait_ge(gelu, 6 * s + m + 1)
                nc.scalar.copy(hT[:, m, 0, :], h32[:, m, :]).then_inc(h_hi, 1)

            def q_rounded(b, s):
                for j in range(2):
                    act.wait_ge(fill, FILLS * s + 9 + j)
                    nc.scalar.activation(qT[b][:, 0, j, :], ring[(8 + j) % 3][:, :], ACT.Identity,
                                         bias=b2c[:, Q, j:j + 1]).then_inc(q_hi, 1)

            def k_rounded(s):
                for j in range(2):
                    act.wait_ge(fill, FILLS * s + 11 + j)
                    nc.scalar.activation(k32[:, j, :], ring[(10 + j) % 3][:, :], ACT.Identity,
                                         bias=b2c[:, K, j:j + 1]).then_inc(k_full, 1)
                    act.wait_ge(k_full, 2 * s + 1 + j)
                    nc.scalar.copy(kT[:, 0, j, :], k32[:, j, :]).then_inc(k_hi, 1)

            def v_rounded(b, s):
                for j in range(2):
                    act.wait_ge(v_sum, 2 * s + 1 + j)
                    nc.scalar.copy(vtok[b][:, 0, 2 * j:2 * j + 2, :], v32[:, 2 * j:2 * j + 2, :]).then_inc(v_hi, 1)

            def scores_rounded(s):
                act.wait_ge(sc_mask, s + 1)
                nc.scalar.copy(scT[:, 0, :], sc32[:, :]).then_inc(sc_hi, 1)

            def ktok_rounded(b, s):
                for n in range(2):
                    act.wait_ge(fill, FILLS * s + 15 + n)
                    nc.scalar.copy(ktok[b][:, 0, 2 * n:2 * n + 2, :],
                                   ring[(14 + n) % 3][:, :].rearrange("p (c d) -> p c d", c=2)
                                   ).then_inc(ktok_hi, 1)

            def state_rounded(b, s, c):
                act.wait_ge(s_ready, 4 * s + c + 1)
                nc.scalar.copy(state[b][:, 0, :], s_ps[b][:, :]).then_inc(s_hi, 1)

            def tile_rounded(ts):
                for t in ts:
                    act.wait_ge(wf_t, t + 1)
                    nc.scalar.copy(wf_sp[:, t, 0, :], ring[t % 3][:, :]).then_inc(wf_hi, 1)

            def body(g, b, front, lead, fillers=None):
                s = NB * g + b
                if front:
                    xnT_rounded(s + 1)
                state_rounded(b, s, 0)
                for c in range(1, CH):
                    if front:
                        for m in (2 * c - 2, 2 * c - 1):
                            gelus(s + 1, (m,))
                            h_rounded(s + 1, m)
                    elif fillers:
                        fillers(c - 1)
                    if front or c < CH - 1:
                        state_rounded(b, s, c)
                if front:
                    q_rounded(1 - b, s + 1)
                    k_rounded(s + 1)
                    v_rounded(1 - b, s + 1)
                    ktok_rounded(1 - b, s + 1)
                    scores_rounded(s + 1)

            for i in range(6):
                if i < 3:
                    act.wait_ge(w_in[i], 16)
                else:
                    act.wait_ge(w_scaled, 1)
                    act.wait_ge(w_in[i], 16)
                nc.scalar.copy(w_sp[:, i, 0, :, :], w_stage[:, i, :, :]).then_inc(w_hi, 1)
                if i == 2:
                    xnT_rounded(0)
            act.wait_ge(small_in, 32)
            act.wait_ge(rp, 1)
            for m in range(6):
                gelus(0, (m,))
                h_rounded(0, m)
            q_rounded(0, 0)
            k_rounded(0)
            v_rounded(0, 0)
            ktok_rounded(0, 0)
            scores_rounded(0)
            with act.Fori(0, STEPS // NB - 1) as g:
                for b in range(NB):
                    body(g, b, True, True)
            body(STEPS // NB - 1, 0, True, False)

            def fillers(n):
                if n == 0:
                    tile_rounded(range(3))
                if n == 1:
                    act.wait_ge(bias_in, 32)
                    for i in range(2):
                        nc.scalar.copy(bias_hl[:, i, :], bias_raw[i]).then_inc(bias_hi, 1)

            body(STEPS // NB - 1, 1, False, False, fillers)
            tile_rounded(range(3, NT))

            def block_norm(turn, p, first):
                n = RB * turn + p
                k = act.value_load(pair_i[0:1, 1, bass.ds(n, 1)], min_val=0, max_val=NJ - 1)
                act.wait_ge(rows_in, n + 1)
                if not first:
                    act.wait_ge(xb_t, n - RB + 1)
                for b in range(NB):
                    r = rows[:, bass.ds(k, 1), b * ROW:(b + 1) * ROW].rearrange("p k d -> p (k d)")
                    last = nc.scalar.activation(xnb[p][:, b, :], r[:, 0:C], ACT.Identity, bias=r[:, C:C + 1],
                                                scale=r[:, C + 1:C + 2])
                last.then_inc(xnb_done, 1)

            def block_rounded(n, p):
                act.wait_ge(xb_t, n + 1)
                nc.scalar.copy(xbT[p][:, 0, :], t_bank[p][:, :]).then_inc(xb_hi, 1)

            act.wait_ge(rp, 3)
            act.wait_ge(rv, ROUTED)
            block_norm(0, 0, True)
            block_norm(0, 1, True)

            def one_slot(turn, j, edge):
                n = RB * turn + j
                if not edge or n < NPAIR:
                    block_rounded(n, j)
                if not edge or n + 2 < NPAIR:
                    block_norm(turn + (j + 2) // RB, (j + 2) % RB, edge and n + 2 < RB)

            over_slots(act, one_slot)

        @block.vector
        def _(dve):
            def lead_stat(g, b, c):
                if c == 0:
                    dve.wait_ge(x_in[b], 16 * (g + 1))
                nc.vector.bn_stats(st1[:, c, :], xt[b][:, c, :]).then_inc(stat1, 1)

            def lead_var(g, b):
                s = NB * g + b
                dve.wait_ge(stat1, CH * s + CH)
                alone(dve, gate_dve)
                for c in range(CH):
                    last = nc.vector.bn_aggr(mv1[:, c, :], st1[:, c, :])
                last.then_inc(aggr1, 1)
                dve.wait_ge(aggr1, s + 1)
                nc.vector.tensor_scalar(ve1[:, :], mv1[:, :, 1], EPS, None, ALU.add).then_inc(var1, 1)

            def lead_norm(g, b, first):
                s = NB * g + b
                dve.wait_ge(rstd1, s + 1)
                if not first:
                    dve.wait_ge(fill, FILLS * (s - 1) + 2)
                for c in range(CH):
                    last = nc.vector.tensor_scalar(xn[:, c, :], xt[b][:, c, :], mv1[:, c, 0:1], rs1[:, c:c + 1],
                                                   ALU.subtract, ALU.mult)
                last.then_inc(xn_done, 1)

            def xnT_rest(s):
                for k in range(KC):
                    dve.wait_ge(xnT_hi, 2 * s + 1 + k)
                    nc.vector.tensor_tensor(xnT[:, 1, k, :], ring[k][:, :], xnT[:, 0, k, :].bitcast(F32),
                                            ALU.subtract).then_inc(xnT_lo, 1)

            def h_rest(s, m):
                dve.wait_ge(h_hi, 6 * s + m + 1)
                nc.vector.tensor_tensor(hT[:, m, 1, :], h32[:, m, :], hT[:, m, 0, :].bitcast(F32),
                                        ALU.subtract).then_inc(h_lo_dve, 1)

            def q_rest(b, s):
                for j in range(2):
                    dve.wait_ge(q_hi, 2 * s + 1 + j)
                    nc.vector.scalar_tensor_tensor(out=qT[b][:, 1, j, :], in0=ring[(8 + j) % 3][:, :],
                                                   scalar=b2c[:, Q, j:j + 1], in1=qT[b][:, 0, j, :].bitcast(F32),
                                                   op0=ALU.add, op1=ALU.subtract).then_inc(q_lo, 1)

            def k_rest(s):
                for j in range(2):
                    dve.wait_ge(k_hi, 2 * s + 1 + j)
                    nc.vector.tensor_tensor(kT[:, 1, j, :], k32[:, j, :], kT[:, 0, j, :].bitcast(F32),
                                            ALU.subtract).then_inc(k_lo, 1)

            def ktok_rest(b, s):
                for n in range(2):
                    dve.wait_ge(ktok_hi, 2 * s + 1 + n)
                    nc.vector.tensor_tensor(ktok[b][:, 1, 2 * n:2 * n + 2, :],
                                            ring[(14 + n) % 3][:, :].rearrange("p (c d) -> p c d", c=2),
                                            ktok[b][:, 0, 2 * n:2 * n + 2, :].bitcast(F32),
                                            ALU.subtract).then_inc(ktok_lo, 1)

            def v_biased(s, j):
                dve.wait_ge(fill, FILLS * s + 13 + j)
                nc.vector.tensor_tensor(v32[:, 2 * j:2 * j + 2, :], ring[j][:, :].rearrange("p (c d) -> p c d", c=2),
                                        b2v_row[:, :].unsqueeze(1).broadcast_to([P, 2, C]),
                                        ALU.add).then_inc(v_sum, 1)

            def scores_masked(s):
                dve.wait_ge(scores, s + 1)
                nc.vector.tensor_tensor(sc32[:, :].rearrange("p (c i) -> p c i", c=CH),
                                        sc_ps[:, :].rearrange("p (c i) -> p c i", c=CH),
                                        tril[:, :].unsqueeze(1).broadcast_to([P, CH, P]), ALU.mult).then_inc(sc_mask, 1)

            def scores_rest(s):
                dve.wait_ge(sc_hi, s + 1)
                nc.vector.tensor_tensor(scT[:, 1, :], sc32[:, :], scT[:, 0, :].bitcast(F32),
                                        ALU.subtract).then_inc(sc_lo, 1)

            def state_rest(b, s, c):
                dve.wait_ge(s_hi, 4 * s + c + 1)
                nc.vector.tensor_tensor(state[b][:, 1, :], s_ps[b][:, :], state[b][:, 0, :].bitcast(F32),
                                        ALU.subtract).then_inc(s_lo, 1)

            def out_centred(s, c):
                o = o_ps[c % 2][:, 0:C]
                dve.wait_ge(o_ready, 4 * s + c + 1)
                nc.vector.bn_stats(st2[:, c, :], o).then_inc(o_stat, 1)
                dve.wait_ge(o_stat, 4 * s + c + 1)
                alone(dve, gate_dve)
                nc.vector.bn_aggr(mv2[:, c, :], st2[:, c, :]).then_inc(o_aggr, 1)
                dve.wait_ge(o_aggr, 4 * s + c + 1)
                nc.vector.scalar_tensor_tensor(out=cen[:, c, :], in0=o, scalar=mv2[:, c, 0:1], in1=lnw_row[:, :],
                                               op0=ALU.subtract, op1=ALU.mult).then_inc(o_cen, 1)

            def out_var(cs=slice(0, CH)):
                nc.vector.tensor_scalar(ve2[:, cs], mv2[:, cs, 1], EPS, None, ALU.add).then_inc(var2, 1)

            def x1_final(g, b, cs, part=0):
                s = NB * g + b
                if cs[0] == 0 or part:
                    dve.wait_ge(rstd2, s + 1 + part)
                    dve.wait_ge(res_done, s + 1)
                for c in cs:
                    nc.vector.scalar_tensor_tensor(out=xres[b][:, c, 0:C], in0=cen[:, c, :],
                                                   scalar=rs2[:, c:c + 1], in1=xres[b][:, c, 0:C],
                                                   op0=ALU.mult, op1=ALU.add).then_inc(x1_made, 1)

            def x1_stats(g, b, cs=range(CH)):
                dve.wait_ge(x1_made, CH * (NB * g + b) + cs[-1] + 1)
                for c in cs:
                    last = nc.vector.bn_stats(st3[:, c, :], xres[b][:, c, 0:C])
                last.then_inc(stat3, 1)

            def x1_var(g, b, cs=range(CH), part=0):
                s = NB * g + b + part
                dve.wait_ge(stat3, s + 1)
                alone(dve, gate_dve)
                for c in cs:
                    last = nc.vector.bn_aggr(mv3[:, c, :], st3[:, c, :])
                last.then_inc(aggr3, 1)
                dve.wait_ge(aggr3, s + 1)
                cs = slice(cs[0], cs[-1] + 1)
                nc.vector.tensor_scalar(nm3[:, cs], mv3[:, cs, 0], -1.0, None, ALU.mult)
                nc.vector.tensor_scalar(ve3[:, cs], mv3[:, cs, 1], EPS, None, ALU.add).then_inc(var3, 1)

            def body(g, b, front, lead, fillers=None):
                s = NB * g + b
                for c in range(1, CH - 1):
                    state_rest(b, s, c)
                    out_centred(s, c)
                    if fillers:
                        fillers(c - 1)
                    if lead and c == 1:
                        for i in range(CH):
                            lead_stat(g + 1, b, i)
                        lead_var(g + 1, b)
                    if lead and c == 2:
                        lead_norm(g + 1, b, False)
                    if front:
                        h_rest(s + 1, 2 * c - 2)
                out_centred(s, CH - 1)
                out_var()
                if front:
                    h_rest(s + 1, 4)
                    q_rest(1 - b, s + 1)
                state_rest(b, s, CH - 1)
                x1_final(g, b, (0, 1))
                if front:
                    k_rest(s + 1)
                    v_biased(s + 1, 0)
                    v_biased(s + 1, 1)
                    if fillers:
                        fillers(2)
                    ktok_rest(1 - b, s + 1)
                    scores_masked(s + 1)
                x1_final(g, b, (2,))
                if front:
                    scores_rest(s + 1)
                if lead:
                    xnT_rest(s + 2)
                if front:
                    state_rest(1 - b, s + 1, 0)
                    out_centred(s + 1, 0)
                x1_final(g, b, (3,))
                if front and not lead:
                    tile_rest((0,))
                    route_pair_ranges()
                    state_rest(1 - b, s + 1, 1)
                    out_centred(s + 1, 1)
                x1_stats(g, b)
                x1_var(g, b)

            done = [0]

            def link(ins):
                done[0] += 1
                ins.then_inc(rv, 1)
                dve.wait_ge(rv, done[0])

            def tile_rest(ts):
                for t in ts:
                    dve.wait_ge(wf_hi, t + 1)
                    nc.vector.tensor_tensor(wf_sp[:, t, 1, :], ring[t % 3][:, :], wf_sp[:, t, 0, :].bitcast(F32),
                                            ALU.subtract).then_inc(wf_lo, 1)

            def over_t(a):
                return a.unsqueeze(1).broadcast_to([P, NT, NJ])

            def over_j(a):
                return a.unsqueeze(2).broadcast_to([P, NT, NJ])

            def by_j(a):
                return a.rearrange("p t j -> p j t")

            def route_signs():
                dve.wait_ge(sigs_in, 16)
                link(nc.vector.tensor_scalar(sgn[:, 0, :], sig_in[:, :], 0.0, None, ALU.is_gt))
                link(nc.vector.tensor_scalar(sgn[:, 1, :], sig_in[:, :], 0.0, None, ALU.is_lt))
                link(nc.vector.tensor_tensor(sgn_r[:, :], sgn[:, 0, :], sgn[:, 1, :], ALU.subtract))

            def route_argmax():
                dve.wait_ge(rp, 1)
                dve.wait_ge(rconst, 7)
                link(nc.vector.tensor_copy(rsc[:, :, :], sc_ps[:, 0:NJ * NT].rearrange("p (j t) -> p t j", t=NT)))
                link(nc.vector.tensor_reduce(rmax[:, :], by_j(rsc[:, :, :]), AX_X, ALU.max))
                link(nc.vector.tensor_tensor(req[:, :, :], rsc[:, :, :], over_t(rmax[:, :]), ALU.is_ge))
                link(nc.vector.tensor_tensor(rcand[:, :, :], req[:, :, :], revt[:, :, :], ALU.mult))
                link(nc.vector.tensor_reduce(rbest[:, :], by_j(rcand[:, :, :]), AX_X, ALU.max))
                link(nc.vector.tensor_tensor(onehot[:, :, :], revt[:, :, :], over_t(rbest[:, :]), ALU.is_equal))

            def route_ranks():
                dve.wait_ge(rp, 2)
                link(nc.vector.tensor_copy(ranks[:, :, :, :].rearrange("p a t j -> p (a t j)"), sc_ps[:, 128:384]))

            def route_starts():
                tot = ranks[:, 1]
                link(nc.vector.tensor_tensor_scan(incl[:, :, :].rearrange("p t j -> p (t j)"),
                                                  keep[:, :, :].rearrange("p t j -> p (t j)"),
                                                  tot.rearrange("p t j -> p (t j)"), 0.0,
                                                  ALU.mult, ALU.add))
                link(nc.vector.tensor_tensor_scan(ends, keep8[:, :], incl[:, :, NJ - 1], 0.0, ALU.mult, ALU.add))
                link(nc.vector.tensor_tensor(starts, ends, incl[:, :, NJ - 1], ALU.subtract))
                link(nc.vector.tensor_tensor(zed[:, :, :], incl[:, :, :], tot, ALU.subtract))
                link(nc.vector.tensor_tensor(zed[:, :, :], zed[:, :, :], over_j(starts), ALU.add))
                link(nc.vector.tensor_tensor(zed[:, :, :], ranks[:, 0], zed[:, :, :], ALU.add))

            def route_slots():
                link(nc.vector.tensor_tensor(slot_t[:, :, :], zed[:, :, :], onehot[:, :, :], ALU.mult))
                link(nc.vector.tensor_reduce(slot[:, :], by_j(slot_t[:, :, :]), AX_X, ALU.add))
                dve.wait_ge(rconst, 8)
                link(nc.vector.tensor_tensor(above[:, :, :], slot[:, :].unsqueeze(2).broadcast_to([P, NJ, NJ + 1]),
                                             edges[:, :, :], ALU.is_ge))
                link(nc.vector.tensor_reduce(nblk[:, :], above[:, :, 1:NJ], AX_X, ALU.add))
                link(nc.vector.scalar_tensor_tensor(out=rest[:, :], in0=nblk[:, :], scalar=-float(P), in1=slot[:, :],
                                                    op0=ALU.mult, op1=ALU.add))

                link(nc.vector.tensor_tensor(inblk[:, :, :], above[:, :, 0:NJ], above[:, :, 1:NJ + 1],
                                             ALU.subtract))
                link(nc.vector.tensor_tensor(poscol[:, :, :], inblk[:, :, :],
                                             posn[:, :].unsqueeze(2).broadcast_to([P, NJ, NJ]), ALU.mult))

            def route_rows():
                dve.wait_ge(rp, 3)
                link(nc.vector.tensor_copy(idx_i[:, 0], sc_ps[:, 0:NJ]))
                link(nc.vector.tensor_scalar(idx_i[:, 1], sc_ps[:, 0:NJ], float(T), None, ALU.add))

            def route_pairs():
                link(nc.vector.tensor_tensor(blk_gt[:, :, :], over_j(ends), blk_edge[:, :, :], ALU.is_gt))
                link(nc.vector.tensor_reduce(blk_end, blk_gt[:, :, :], AX_X, ALU.add))
                link(nc.vector.tensor_tensor(blk_gt[:, :, :], over_j(starts), blk_edge[:, :, :], ALU.is_ge))
                link(nc.vector.tensor_reduce(blk_first, blk_gt[:, :, :], AX_X, ALU.add))
                link(nc.vector.scalar_tensor_tensor(out=pairs8, in0=blk_end, scalar=1.0, in1=blk_first,
                                                    op0=ALU.add, op1=ALU.subtract))

            def route_pair_ranges():
                link(nc.vector.tensor_tensor_scan(upto8, keep8[:, :], pairs8, 0.0, ALU.mult, ALU.add))
                link(nc.vector.tensor_tensor(before8, upto8, pairs8, ALU.subtract))
                link(nc.vector.scalar_tensor_tensor(out=base8, in0=blk_first, scalar=-1.0, in1=before8,
                                                    op0=ALU.add, op1=ALU.subtract))

            def route_pair_values():
                for i, edge in enumerate((before8, upto8)):
                    link(nc.vector.tensor_tensor(pge[:, i], pcol[:, :, :],
                                                 edge.unsqueeze(1).broadcast_to([P, NPAIR, NT]), ALU.is_ge))
                link(nc.vector.tensor_tensor(pair_t[:, :, :], pge[:, 0], pge[:, 1], ALU.subtract))
                for q in range(4):
                    ins = nc.vector.tensor_tensor(pair_m[:, q], pair_t[:, :, :],
                                                  tile_q[:, q].unsqueeze(1).broadcast_to([P, NPAIR, NT]), ALU.mult)
                link(ins)
                link(nc.vector.tensor_reduce(pair_q[:, :, :], pair_m[:, :, :, :], AX_X, ALU.add))

            def route_tables():
                link(nc.vector.tensor_tensor(pair_f[:, 0], pair_q[:, 2], pcol[:, :, 0], ALU.add))
                link(nc.vector.tensor_scalar(pair_f[:, 1], pair_f[:, 0], float(NJ - 1), None, ALU.min))
                link(nc.vector.tensor_scalar(pair_f[:, 2], pair_f[:, 1], float(P), lane_p[:, :], ALU.mult, ALU.add))
                link(nc.vector.tensor_tensor(pair_f[:, 3], pair_f[:, 2], pair_q[:, 0], ALU.is_ge))
                link(nc.vector.tensor_tensor(pair_f[:, 4], pair_f[:, 2], pair_q[:, 1], ALU.is_ge))
                link(nc.vector.tensor_tensor(mask[:, :], pair_f[:, 3], pair_f[:, 4], ALU.subtract))
                link(nc.vector.tensor_copy(pair_i[:, 0], pair_q[0:1, 3]))
                link(nc.vector.tensor_copy(pair_i[:, 1], pair_f[0:1, 1]))

            for b in range(NB):
                nc.vector.memset(s_ps[b][:, :], 0.0).then_inc(zeroed, 1)
            for b in range(NB):
                last = nc.vector.memset(state[b][:, :, :].bitcast(F32), 0.0)
            last.then_inc(s_lo, 1)
            dve.sem_inc(o_cen, 2)
            for c in range(CH):
                lead_stat(0, 0, c)
            lead_var(0, 0)
            route_signs()
            lead_norm(0, 0, True)

            def weights_rest(ws):
                for i in ws:
                    dve.wait_ge(w_hi, i + 1)
                    nc.vector.tensor_tensor(w_sp[:, i, 1, :, :], w_stage[:, i, :, :],
                                            w_sp[:, i, 0, :, :].bitcast(F32), ALU.subtract).then_inc(w_lo, 1)

            weights_rest((0, 1))
            xnT_rest(0)
            weights_rest((2,))
            dve.wait_ge(w_in[3], 16)
            nc.vector.tensor_scalar(w_stage[:, 3, :, :], w_stage[:, 3, :, :], INV_SCALE, None,
                                    ALU.mult).then_inc(w_scaled, 1)
            weights_rest((3, 4, 5))
            dve.wait_ge(small_in, 32)
            nc.vector.tensor_scalar(b2c[:, Q, :], b2c[:, Q, :], INV_SCALE, None, ALU.mult).then_inc(w_scaled, 1)
            for c in range(CH):
                lead_stat(0, 1, c)
            lead_var(0, 1)
            h_rest(0, 0)
            route_argmax()
            for m in (2, 4):
                h_rest(0, m)
            route_ranks()
            dve.wait_ge(w_scaled, 2)
            q_rest(0, 0)
            lead_norm(0, 1, False)
            k_rest(0)
            v_biased(0, 0)
            v_biased(0, 1)
            ktok_rest(0, 0)
            dve.wait_ge(consts, 4)
            scores_masked(0)
            scores_rest(0)
            xnT_rest(1)
            state_rest(0, 0, 0)
            out_centred(0, 0)
            with dve.Fori(0, STEPS // NB - 1) as g:
                for b in range(NB):
                    body(g, b, True, True)
            def route_more(n):
                (route_starts, route_slots, route_pairs)[n]()

            body(STEPS // NB - 1, 0, True, False, route_more)

            g, b, s = STEPS // NB - 1, NB - 1, STEPS - 1
            state_rest(b, s, 2)
            out_centred(s, 2)
            out_var(slice(0, CH - 1))
            tile_rest((1, 2))
            x1_final(g, b, range(CH - 1))
            out_centred(s, CH - 1)
            out_var(slice(CH - 1, CH))
            x1_stats(g, b, range(CH - 1))
            x1_var(g, b, range(CH - 1))
            route_rows()
            x1_final(g, b, (CH - 1,), 1)
            x1_stats(g, b, (CH - 1,))
            x1_var(g, b, (CH - 1,), 1)
            route_pair_values()
            tile_rest((3, 4, 5))
            route_tables()
            tile_rest((6, 7))

            def block_rest(n, p):
                dve.wait_ge(xb_hi, n + 1)
                nc.vector.tensor_tensor(xbT[p][:, 1, :], t_bank[p][:, :], xbT[p][:, 0, :].bitcast(F32),
                                        ALU.subtract).then_inc(xb_lo, 1)

            def block_out(n, p, first):
                k = dve.value_load(pair_i[0:1, 1, bass.ds(n, 1)], min_val=0, max_val=NJ - 1)
                dve.wait_ge(copied, n + 1)
                if not first:
                    dve.wait_ge(y_done, n)
                dve.wait_ge(y_ps, n + 1)
                result = acc[:, bass.ds(k, 1), :].rearrange("p k n -> p (k n)")
                nc.vector.scalar_tensor_tensor(out=result, in0=y_bank[p][:, :], scalar=mask[:, bass.ds(n, 1)],
                                               in1=result, op0=ALU.mult, op1=ALU.add).then_inc(y_done, 1)

            def one_slot(turn, j, edge):
                n = RB * turn + j
                if not edge or n < NPAIR:
                    block_rest(n, j)
                if not edge or n > 0:
                    block_out(n - 1, (j - 1) % RB, edge and n == 1)

            over_slots(dve, one_slot)

        @block.gpsimd
        def _(pool):
            pool.dma_start(peT, pe).then_inc(table_in, 16)
            nc.gpsimd.memset(ident[:, :], 0.0).then_inc(consts, 1)
            pool.wait_ge(consts, 1)
            nc.gpsimd.affine_select(out=ident[:, :], in_=ident[:, :], compare_op=ALU.not_equal, fill=1.0, base=0,
                                    pattern=[[-1, P]], channel_multiplier=1).then_inc(consts, 1)
            nc.gpsimd.memset(half[:, :], -0.5).then_inc(consts, 1)
            nc.gpsimd.memset(tril[:, :], 1.0).then_inc(rconst, 1)
            pool.wait_ge(rconst, 1)

            def rstd_lead(s):
                pool.wait_ge(var1, s + 1)
                nc.gpsimd.tensor_tensor(rs1[:, :], ve1[:, :], half[:, :], ALU.pow).then_inc(rstd1, 1)

            def residual(g, b, first):
                pool.wait_ge(x_in[b], 16 * (g + 1))
                if not first:
                    pool.wait_ge(x1_out[b], 16 * (g + b))
                nc.gpsimd.tensor_tensor(xres[b][:, :, 0:C], xt[b][:, :, :],
                                        lnb_row[:, :].unsqueeze(1).broadcast_to([P, CH, C]),
                                        ALU.add).then_inc(res_done, 1)

            def h_rest(s, m):
                pool.wait_ge(h_hi, 6 * s + m + 1)
                nc.gpsimd.tensor_tensor(hT[:, m, 1, :], h32[:, m, :], hT[:, m, 0, :].bitcast(F32),
                                        ALU.subtract).then_inc(h_lo_pool, 1)

            def v_rest(b, s):
                for j in range(2):
                    pool.wait_ge(v_hi, 2 * s + 1 + j)
                    nc.gpsimd.tensor_tensor(vtok[b][:, 1, 2 * j:2 * j + 2, :], v32[:, 2 * j:2 * j + 2, :],
                                            vtok[b][:, 0, 2 * j:2 * j + 2, :].bitcast(F32),
                                            ALU.subtract).then_inc(v_lo, 1)

            def rstd_out(s, cs=slice(0, CH)):
                pool.wait_ge(var2, s + 1)
                nc.gpsimd.tensor_tensor(rs2[:, cs], ve2[:, cs], half[:, cs], ALU.pow).then_inc(rstd2, 1)

            def rstd_x1(b, s, cs=slice(0, CH)):
                pool.wait_ge(var3, s + 1)
                nc.gpsimd.tensor_tensor(xres[b][:, cs, C + 1], ve3[:, cs], half[:, cs], ALU.pow).then_inc(rstd3, 1)
                pool.wait_ge(rstd3, s + 1)
                nc.gpsimd.tensor_tensor(xres[b][:, cs, C], nm3[:, cs], xres[b][:, cs, C + 1], ALU.mult
                                        ).then_inc(shift3, 1)

            def lane_onehots(js):
                for j in js:
                    nc.gpsimd.tensor_scalar(lane_oh[j], lane[:, :], rest[:, j:j + 1], None, ALU.is_equal).then_inc(lanes, 1)

            def bias_rest(i):
                pool.wait_ge(lanes, NJ)
                pool.wait_ge(bias_hi, i + 1)
                nc.gpsimd.tensor_tensor(bias_hl[LOW:LOW + 1, i, :], bias_raw[i][LOW:LOW + 1, :],
                                        bias_hl[LOW:LOW + 1, i, :].bitcast(F32), ALU.subtract).then_inc(bias_lo, 1)
                pool.wait_ge(bias_lo, i + 1)

            def body(g, b, front, lead, lanes_too=False):
                s = NB * g + b
                if lead:
                    rstd_lead(s + 2)
                if front:
                    h_rest(s + 1, 1)
                    residual(g + b, 1 - b, False)
                    h_rest(s + 1, 3)
                    h_rest(s + 1, 5)
                rstd_out(s)
                if lanes_too:
                    pool.wait_ge(rv, 21)
                    pool.wait_ge(fill, FILLS * (s + 1) + 2)
                    lane_onehots(range(NJ // 2))
                if front:
                    v_rest(1 - b, s + 1)
                if lanes_too:
                    pool.wait_ge(v_lo, 2 * (s + 2))
                    lane_onehots(range(NJ // 2, NJ))
                    bias_rest(0)
                rstd_x1(b, s)

            pool.wait_ge(consts, 3)
            rstd_lead(0)
            nc.gpsimd.affine_select(out=tril[:, :], in_=tril[:, :], compare_op=ALU.is_ge, fill=0.0, base=0,
                                    pattern=[[1, P]], channel_multiplier=-1).then_inc(consts, 1)
            nc.gpsimd.memset(ones[:, :], 1.0).then_inc(rconst, 1)
            nc.gpsimd.memset(keep8[:, :], 1.0)
            nc.gpsimd.memset(keep[:, :, :], 1.0).then_inc(rconst, 1)
            pool.wait_ge(rconst, 3)
            nc.gpsimd.memset(keep[:, :, 0:1], 0.0).then_inc(rconst, 1)
            nc.gpsimd.affine_select(out=lower[:, :], in_=ones[:, :], compare_op=ALU.is_gt, fill=0.0, base=0,
                                    pattern=[[1, P]], channel_multiplier=-1).then_inc(rconst, 1)
            exact = dict(allow_small_or_imprecise_dtypes=True)
            nc.gpsimd.iota(revt[:, :, :], [[-1, NT], [0, NJ]], base=NT, channel_multiplier=0, **exact)
            nc.gpsimd.iota(blk_edge[:, :, :], [[0, NT], [P, NJ]], base=0, channel_multiplier=0, **exact
                           ).then_inc(rconst, 1)
            nc.gpsimd.iota(lane[:, :], [[1, P]], base=0, channel_multiplier=0, **exact)
            nc.gpsimd.iota(lane_p[:, :], [[0, 1]], base=0, channel_multiplier=1, **exact)
            nc.gpsimd.iota(number8, [[1, NT]], base=0, channel_multiplier=0, **exact)
            nc.gpsimd.iota(posn[:, :], [[P, NJ]], base=0, channel_multiplier=1, **exact).then_inc(rconst, 1)
            pool.wait_ge(small_in, 32)
            residual(0, 0, True)
            pool.wait_ge(w_lo, 6)
            nc.gpsimd.iota(edges[:, :, :], [[0, NJ], [P, NJ + 1]], base=0, channel_multiplier=0, **exact)
            nc.gpsimd.iota(pcol[:, :, :], [[1, NPAIR], [0, NT]], base=0, channel_multiplier=0, **exact
                           ).then_inc(rconst, 1)
            rstd_lead(1)
            pool.sem_inc(x1_out[1], 16)
            for m in (1, 3, 5):
                h_rest(0, m)
            v_rest(0, 0)
            nc.gpsimd.memset(ones_r[:, :].bitcast(F32), 0.0).then_inc(ones_set, 1)
            pool.wait_ge(ones_set, 1)
            nc.gpsimd.memset(ones_r[0:1, :].bitcast(F32), 1.0).then_inc(ones_set, 1)
            pool.wait_ge(ones_set, 2)
            nc.gpsimd.memset(ones_r[LOW:LOW + 1, :].bitcast(F32), 1.0).then_inc(ones_set, 1)
            pool.wait_ge(ones_set, 3)
            with pool.Fori(0, STEPS // NB - 1) as g:
                for b in range(NB):
                    body(g, b, True, True)

            body(STEPS // NB - 1, 0, True, False, True)
            parts = (slice(0, CH - 1), slice(CH - 1, CH))
            rstd_out(STEPS - 1, parts[0])
            pool.wait_ge(rstd2, STEPS)
            bias_rest(1)
            rstd_out(STEPS, parts[1])
            for part in range(2):
                rstd_x1(NB - 1, STEPS - 1 + part, parts[part])

            pool.wait_ge(rv, ROWS_ROUTED)
            for b in range(NB):
                pool.wait_ge(x1_out[b], 16 * (STEPS // NB + 2 * b))
            for n in range(NJ + RB - 1):
                if n >= RB - 1:
                    pool.wait_ge(got[(n + 1) % RB], 16 * ((n + 1) // RB))
                    pool.sem_inc(rows_in, 1)
                if n < NJ:
                    pool.indirect_dma_start(out=rows[:, n, :], out_offset=None, in_=scratch,
                                            in_offset=bass.IndirectOffsetOnAxis(ap=idx_i[:, 0, n:n + 1], axis=0)
                                            ).then_inc(got[n % RB], 16)
            pool.sem_inc(rows_in, NPAIR - NJ)
            for n in range(NJ):
                pool.wait_ge(y_done, n + NPAIR - NJ + 1)
                for b in range(NB):
                    pool.indirect_dma_start(out=out_rows, out_offset=bass.IndirectOffsetOnAxis(
                                                ap=idx_i[:, b, n:n + 1], axis=0),
                                            in_=acc[:, n, b * C:(b + 1) * C], in_offset=None).then_inc(sent, 16)
            pool.wait_ge(sent, 16 * NB * NJ)


def position_table(seq, dim):
    import math
    import numpy as np
    pos = np.arange(seq, dtype=np.float32)[:, None]
    step = np.arange(0, dim, 2, dtype=np.float32) * np.float32(-math.log(10000.0) / dim)
    angle = (pos * np.exp(step.astype(np.float64)).astype(np.float32)).astype(np.float64)
    table = np.zeros((seq, dim), dtype=np.float32)
    table[:, 0::2] = np.sin(angle)
    table[:, 1::2] = np.cos(angle)
    bits = np.ascontiguousarray(table.T).view(np.uint32)
    hi = ((bits + np.uint32(0x800)) & np.uint32(0xFFFFF000)).view(np.float32)
    return np.concatenate([hi, table.T - hi])


_INS = ['L0_attn_x', 'L0_attn_W1q', 'L0_attn_b1q', 'L0_attn_W2q', 'L0_attn_b2q', 'L0_attn_W1k', 'L0_attn_b1k',
        'L0_attn_W2k', 'L0_attn_b2k', 'L0_attn_W1v', 'L0_attn_b1v', 'L0_attn_W2v', 'L0_attn_b2v', 'L0_attn_ln_w',
        'L0_attn_ln_b', 'L0_ffn_tile_sigs', 'L0_ffn_W', 'L0_ffn_b']


def kernel(**inputs):
    import numpy as _np
    import concourse.bacc as _bacc
    from concourse import mybir as _mybir
    from concourse.bass_utils import run_bass_kernel_spmd as _run

    nc = _bacc.Bacc("TRN2", target_bir_lowering=False, num_devices=1)
    x = {name: _np.ascontiguousarray(inputs[name]) for name in _INS}
    col = lambda name: x[name].reshape(KC, P).T
    arrays = {
        "x": x['L0_attn_x'],
        **{f"w{l}{n}": x[f'L0_attn_W{l}{n}'] for l in (1, 2) for n in 'qkv'},
        "bias_columns": _np.concatenate([col('L0_attn_' + n) for n in ('b1q', 'b1k', 'b1v', 'b2q', 'b2k')], axis=1),
        "rows": _np.stack([x['L0_attn_ln_w'], x['L0_attn_ln_b'], x['L0_attn_b2v']]),
        "tile_sigs": _np.concatenate([x['L0_ffn_tile_sigs'].T] * 2),
        "tile_w": x['L0_ffn_W'],
        "tile_b": x['L0_ffn_b'],
        "position_table": position_table(T, DP),
    }
    arrays = {name: _np.ascontiguousarray(a) for name, a in arrays.items()}
    ap = {name: nc.dram_tensor(name, a.shape, _mybir.dt.from_np(a.dtype), kind="ExternalInput").ap()
          for name, a in arrays.items()}
    out = nc.dram_tensor("out_0_dram", (NB, T, C), F32, kind="ExternalOutput").ap()
    mk_seq_kernel(nc, ap["x"], [ap[f"w1{n}"] for n in 'qkv'], [ap[f"w2{n}"] for n in 'qkv'], ap["bias_columns"],
                  ap["rows"], ap["tile_sigs"], ap["tile_w"], ap["tile_b"], ap["position_table"], out)
    r = _run(nc, [arrays], core_ids=[0])
    return r.results[0]["out_0_dram"]
```
